# Optimizing a Trainium2 kernel written in Bass

```python
import numpy as np
import jax
import jax.numpy as jnp

def _softmax(x, axis=-1):
    return jax.nn.softmax(x, axis=axis)

def _gelu(x):
    return jax.nn.gelu(x, approximate=True)

def _silu(x):
    return jax.nn.silu(x)

def _sigmoid(x):
    return jax.nn.sigmoid(x)

def _layernorm(x, axis=-1, eps=1e-05):
    m = jnp.mean(x, axis=axis, keepdims=True)
    v = jnp.var(x, axis=axis, keepdims=True)
    return (x - m) / jnp.sqrt(v + eps)

def _scatter_add(tgt, idx, src, axis=0):
    return tgt.at[idx].add(src)

def _segment_sum(src, seg, n):
    return jax.ops.segment_sum(src, seg, n)
kernel_name = 'mk_gnn_ffn_d1_gnn_r32_4a70da'

def setup_inputs(seed: int=0):
    np.random.seed(seed)
    _w = jnp.asarray

    def _rec_inputs():
        import jax
        import jax.numpy as jnp
        _gk = jax.random.key(seed)
        x = -0.000125 + 0.9999 * jax.random.normal(jax.random.fold_in(_gk, 1), (2048, 512), jnp.float32)
        src = jax.random.randint(jax.random.fold_in(_gk, 2), (32768,), 0, 2048, jnp.int32)
        dst = jax.random.randint(jax.random.fold_in(_gk, 3), (32768,), 0, 2048, jnp.int32)
        _o = jnp.argsort(dst, stable=True)
        src = src[_o]
        dst = dst[_o]
        edge_weight = jax.random.uniform(jax.random.fold_in(_gk, 12), (32768,), jnp.float32, 0.0, 0.999998)
        return (x, src, dst, edge_weight)
    x, src, dst, edge_weight = _rec_inputs()

    def _L0_gnn_setup():
        import jax, jax.numpy as jnp
        import numpy as np
        N_NODES = 2048
        key = jax.random.key(seed)
        k1, k2, k3, k4, k5 = jax.random.split(key, 5)
        in_dim, out_dim, n_edges = (512, 512, 16384)
        H = jax.random.normal(k1, (N_NODES, in_dim), dtype=jnp.float32)
        stdv = 1.0 / np.sqrt(out_dim)
        W = jax.random.uniform(k2, (in_dim, out_dim), minval=-stdv, maxval=stdv, dtype=jnp.float32)
        bias = jnp.zeros((out_dim,), dtype=jnp.float32)
        edge_row = jax.random.randint(k3, (n_edges,), 0, N_NODES, dtype=jnp.int32)
        edge_col = jax.random.randint(k4, (n_edges,), 0, N_NODES, dtype=jnp.int32)
        edge_val = jax.random.uniform(k5, (n_edges,), dtype=jnp.float32)
        return {'H': H, 'W': W, 'bias': bias, 'edge_row': edge_row, 'edge_col': edge_col, 'edge_val': edge_val}
    _L0_gnn_all = _L0_gnn_setup()
    _L0_gnn_in = {k: v for k, v in _L0_gnn_all.items() if k in ('W', 'bias')}
    del _L0_gnn_all

    def _L0_ffn_setup():
        import jax, jax.numpy as jnp
        import numpy as np
        E = 64
        K = 2
        D = 512
        H = 256
        NSH = 2
        ROUTE_SCALE = 2.5
        CAP = 1024
        STD = 0.02
        key = jax.random.key(seed)
        ks = jax.random.split(key, 8)
        x = jax.random.normal(ks[0], (4, 64, D), dtype=jnp.float32)
        gate_w = jax.random.normal(ks[1], (E, D), dtype=jnp.float32) * STD
        w1 = jax.random.normal(ks[2], (E, D, H), dtype=jnp.float32) * STD
        w3 = jax.random.normal(ks[3], (E, D, H), dtype=jnp.float32) * STD
        w2 = jax.random.normal(ks[4], (E, H, D), dtype=jnp.float32) * STD
        sw1 = jax.random.normal(ks[5], (D, H * NSH), dtype=jnp.float32) * STD
        sw3 = jax.random.normal(ks[6], (D, H * NSH), dtype=jnp.float32) * STD
        sw2 = jax.random.normal(ks[7], (H * NSH, D), dtype=jnp.float32) * STD
        return {'x': x, 'gate_w': gate_w, 'w1': w1, 'w3': w3, 'w2': w2, 'sw1': sw1, 'sw3': sw3, 'sw2': sw2}
    _L0_ffn_all = _L0_ffn_setup()
    _L0_ffn_in = {k: v for k, v in _L0_ffn_all.items() if k in ('gate_w', 'w1', 'w3', 'w2', 'sw1', 'sw3', 'sw2')}
    del _L0_ffn_all
    return {'x': x, 'src': src, 'dst': dst, 'edge_weight': edge_weight, 'L0_gnn_W': _L0_gnn_in['W'], 'L0_gnn_bias': _L0_gnn_in['bias'], 'L0_ffn_gate_w': _L0_ffn_in['gate_w'], 'L0_ffn_w1': _L0_ffn_in['w1'], 'L0_ffn_w3': _L0_ffn_in['w3'], 'L0_ffn_w2': _L0_ffn_in['w2'], 'L0_ffn_sw1': _L0_ffn_in['sw1'], 'L0_ffn_sw3': _L0_ffn_in['sw3'], 'L0_ffn_sw2': _L0_ffn_in['sw2']}

def reference(x, src, dst, edge_weight, L0_gnn_W, L0_gnn_bias, L0_ffn_gate_w, L0_ffn_w1, L0_ffn_w3, L0_ffn_w2, L0_ffn_sw1, L0_ffn_sw3, L0_ffn_sw2):
    import jax
    import jax.numpy as jnp

    def _L0_gnn_ref(H, W, bias, edge_row, edge_col, edge_val):
        import jax, jax.numpy as jnp
        import numpy as np
        N_NODES = 2048
        HW = H @ W
        msgs = edge_val[:, None] * HW[edge_col]
        out = jax.ops.segment_sum(msgs, edge_row, num_segments=N_NODES)
        out = out + bias
        return jax.nn.relu(out)

    def _L0_ffn_ref(x, gate_w, w1, w3, w2, sw1, sw3, sw2):
        import jax, jax.numpy as jnp
        import numpy as np
        E = 64
        K = 2
        D = 512
        H = 256
        NSH = 2
        ROUTE_SCALE = 2.5
        CAP = 1024
        STD = 0.02
        bs, slen, d = x.shape
        xf = x.reshape(-1, d)
        logits = xf @ gate_w.T
        scores = jax.nn.sigmoid(logits.astype(jnp.float32))
        top_scores, top_idx = jax.lax.top_k(scores, K)
        top_scores = top_scores / (top_scores.sum(-1, keepdims=True) + 1e-20)
        top_scores = top_scores * ROUTE_SCALE
        flat_e = top_idx.reshape(-1)
        x_pairs = jnp.repeat(xf, K, axis=0)
        oh = jax.nn.one_hot(flat_e, E, dtype=jnp.int32)
        pos = jnp.take_along_axis(jnp.cumsum(oh, axis=0), flat_e[:, None], axis=1)[:, 0] - 1
        buf = jnp.zeros((E, CAP, d), dtype=xf.dtype).at[flat_e, pos].set(x_pairs, mode='drop')
        h = jax.nn.silu(jnp.einsum('ecd,edh->ech', buf, w1)) * jnp.einsum('ecd,edh->ech', buf, w3)
        y = jnp.einsum('ech,ehd->ecd', h, w2)
        valid = (pos < CAP)[:, None]
        y_pairs = jnp.where(valid, y[flat_e, jnp.minimum(pos, CAP - 1)], 0.0)
        routed = (y_pairs.reshape(-1, K, d) * top_scores[..., None].astype(xf.dtype)).sum(axis=1)
        shared = jax.nn.silu(xf @ sw1) * (xf @ sw3) @ sw2
        return (shared + routed).reshape(bs, slen, d)
    x = x + _L0_gnn_ref(_layernorm(x, axis=-1), L0_gnn_W, L0_gnn_bias, src, dst, edge_weight)
    x = x + _L0_ffn_ref(_layernorm(x, axis=-1)[None], L0_ffn_gate_w, L0_ffn_w1, L0_ffn_w3, L0_ffn_w2, L0_ffn_sw1, L0_ffn_sw3, L0_ffn_sw2)[0]
    return x

_drawn_inputs = setup_inputs


def setup_inputs(seed=0):
    import zlib

    import numpy as np

    out = dict(_drawn_inputs(seed))
    spreads = {'L0_gnn_bias': (0.0, 0.1)}
    factors = {}
    for name, (base, spread) in spreads.items():
        noise = np.random.default_rng([zlib.crc32(name.encode()), seed]).standard_normal(out[name].shape)
        drawn = base * np.exp(spread * noise) if base else spread * noise
        out[name] = jnp.asarray(drawn.astype(out[name].dtype))
    for name, factor in factors.items():
        out[name] = (out[name] * factor).astype(out[name].dtype)
    return out
```

```python
import concourse.bass as bass
from concourse import mybir
from contextlib import ExitStack

fp32 = mybir.dt.float32
f32r = mybir.dt.float32r
bf16 = mybir.dt.bfloat16
i32 = mybir.dt.int32
u32 = mybir.dt.uint32
ALU = mybir.AluOpType
ACT = mybir.ActivationFunctionType
AX = mybir.AxisListType

P = 128
N, D = 2048, 512
E = 32768
EXPERTS, TOPK, H = 64, 2, 256
CAP = 1024
ROUTE_SCALE = 2.5
EPS = 1e-5
TILES = N // P
KD = D // P
KH = H // P
EC = E // P
PAIR = 2
PAIRS = E // (PAIR * P) + TILES
CHUNKS = PAIR * PAIRS
RING = 16
HALF = RING // 2
BLOCK_SHIFT = 7
PAIR_SHIFT = 8
MAX_TILES = EXPERTS + N * TOPK // P
NOWHERE = 127
YROWS = MAX_TILES * P


class Steps:

    def __init__(self, engine, sem):
        self.engine, self.sem, self.base, self.n = engine, sem, 0, 0

    def add(self, instruction):
        instruction.then_inc(self.sem, 1)
        self.n += 1

    def wait(self):
        self.engine.wait_ge(self.sem, self.base + self.n)

    def __call__(self, instruction):
        self.add(instruction)
        self.wait()

    def enter(self, i, per):
        self.before, self.per = self.base + self.n, per
        self.base, self.n = self.before + i * per, 0

    def leave(self, times):
        assert self.n == self.per, (self.n, self.per)
        self.base, self.n = self.before + times * self.per, 0


def build_program(nc, x, src, dst, edge_weight, gnn_w, gnn_bias, gate_w, w1, w3, w2, sw1, sw3, sw2, out):
    ctx = ExitStack()
    with ctx:
        def sb(name, shape, dt):
            return ctx.enter_context(nc.sbuf_tensor(name, shape, dt))

        def sem(name):
            return ctx.enter_context(nc.semaphore(name))

        hw_dram = nc.dram_tensor("hw_dram", [N, D], fp32).ap()
        xn_dram = nc.dram_tensor("xn_dram", [N, D], fp32).ap()
        ys_dram = nc.dram_tensor("ys_dram", [YROWS, D], fp32).ap()

        acc = sb("acc", [P, TILES, D], fp32)
        raw = sb("raw", [P, 4, KD, D], fp32)
        ring = raw[:].rearrange("p a k n -> p (a k) n")
        sw_hi = sb("sw_hi", [P, 3, KD, D], f32r)
        sw_lo = sb("sw_lo", [P, 3, KD, D], f32r)
        gw_hi = sb("gw_hi", [P, KD, D], f32r)
        gw_lo = sb("gw_lo", [P, KD, D], f32r)
        scan = sb("scan", [P, TILES * EC], fp32)
        work = sb("work", [P, TILES * EC], fp32)
        onehot = sb("onehot", [P, TILES * EC], bf16)
        rec = sb("rec", [P, 4, EC], fp32)
        slot_tile = sb("slot_tile", [P, EC], fp32)
        slot_lane = sb("slot_lane", [P, EC], fp32)
        ends = sb("ends", [P, 6, TILES], fp32)
        ends_i = sb("ends_i", [P, TILES], i32)
        pair_tab = sb("pair_tab", [P, TILES + 1], i32)
        scratch = sb("scratch", [P, 8, EC], fp32)
        src_i, dst_i, block_i, lane_i, pos_i = (scratch[:, j].bitcast(i32) for j in range(5))
        ew_f, block_f, pos_f = (scratch[:, j] for j in range(5, 8))
        rows2 = scratch[:].rearrange("p (a s b) k -> p a s (b k)", a=2, s=2)
        hwb, xn = rows2[:, 0], rows2[:, 1]
        sdst = scan[:, 1024:1024 + CHUNKS].bitcast(u32)
        slane = scan[:, 1024 + CHUNKS:1024 + 2 * CHUNKS]
        sew = scan[:, 1024 + 2 * CHUNKS:1024 + 3 * CHUNKS]
        logits = scan[:, 2048:2048 + TILES * EXPERTS].rearrange("p (t e) -> p t e", t=TILES)
        iota_i = scan[:, 0:CHUNKS].bitcast(i32)
        gw_hi_flat, gw_lo_flat = (t[:].rearrange("p k n -> p (k n)") for t in (gw_hi, gw_lo))
        lane_oh = gw_hi_flat[:, 0:8 * P].rearrange("p (s f n) -> p s f n", s=2, f=4)
        tile_oh = gw_lo_flat[:, 0:2 * CHUNKS].rearrange("p (s n) -> p s n", s=2)
        g_hi = gw_hi_flat[:, 0:2 * D].rearrange("p (s n) -> p s n", s=2)
        g_lo = gw_lo_flat[:, 0:2 * D].rearrange("p (s n) -> p s n", s=2)
        row_oh = gw_hi_flat[:, 2 * D:2 * D + 2 * P].rearrange("p (s n) -> p s n", s=2)
        ht_hi = gw_hi_flat[:, 3 * D:4 * D].rearrange("p (k n) -> p k n", k=KD)
        ht_lo = gw_lo_flat[:, 3 * D:4 * D].rearrange("p (k n) -> p k n", k=KD)
        route = ring[:, HALF:RING].rearrange("p r n -> p (r n)")
        top8 = route[:, 0:128].rearrange("p (t j) -> p t j", t=TILES)
        idx8 = route[:, 128:256].bitcast(u32).rearrange("p (t j) -> p t j", t=TILES)
        r_small = route[:, 256:576].rearrange("p (j k t) -> p j k t", j=10, k=TOPK)
        r_int = route[:, 576:672].bitcast(i32).rearrange("p (j k t) -> p j k t", j=3, k=TOPK)
        x_small = route[:, 1024:1536].rearrange("p (j e) -> p j e", j=8)
        x_int = route[:, 1536:1600].bitcast(i32)
        stage = sb("stage", [P, 2, HALF], u32)
        bias_hi = sb("bias_hi", [1, D], f32r)
        bias_lo = sb("bias_lo", [1, D], f32r)
        gt_hi = sb("gt_hi", [P, KD, EXPERTS], f32r)
        gt_lo = sb("gt_lo", [P, KD, EXPERTS], f32r)
        xt_hi = sb("xt_hi", [P, 2, KD, P], f32r)
        ew_r = xt_hi[:, 0, 0:EC // P, :].rearrange("p k n -> p (k n)")
        xt_lo = sb("xt_lo", [P, 2, KD, P], f32r)
        hid = sb("hid", [P, 2, D], fp32)
        gate_f = hid[0:EXPERTS, 0]
        bias_f = hid[0:1, 1]
        stats = sb("stats", [P, TILES, 6], fp32)
        mv = sb("mv", [P, TILES, 2], fp32)
        rstd = sb("rstd", [P, TILES], fp32)
        sdev = sb("sdev", [P, TILES], fp32)
        comb_idx = sb("comb_idx", [P, TILES, TOPK], u32)
        tok_sorted = sb("tok_sorted", [P, NOWHERE + 1], u32)
        texp_f = sb("texp_f", [P, 2], fp32)
        texp_row = sb("texp_row", [1, P], i32)
        groups = sb("groups", [P, 1], i32)
        ident = sb("ident", [P, P], fp32)
        before_neg = sb("before_neg", [P, P], bf16)
        ones_b = sb("ones_b", [P, P], bf16)
        one_f = sb("one_f", [1, P], fp32)
        one_r = sb("one_r", [1, P], f32r)
        iota_f = sb("iota_f", [P, CHUNKS], fp32)
        tok_i = sb("tok_i", [P, TILES], i32)
        tok_f = sb("tok_f", [P, TILES], fp32)
        zeros = sb("zeros", [P, D], bf16)
        zeros_r = sb("zeros_r", [P, CHUNKS], f32r)
        eps_t = sb("eps_t", [P, 1], fp32)

        w_raw = [t[:, 0:KD * 2 * H + KH * D] for t in (scan, work)]
        w13_raw = [w[:, 0:KD * 2 * H].rearrange("p (m k n) -> p m k n", m=2, k=KD) for w in w_raw]
        w2_raw = [w[:, KD * 2 * H:].rearrange("p (k n) -> p k n", k=KH) for w in w_raw]

        def split_views(t):
            flat = t[:].rearrange("p a k n -> p (a k n)")
            n = KD * 2 * H + KH * D
            return ([flat[:, s * n:s * n + KD * 2 * H] for s in range(2)],
                    [flat[:, s * n + KD * 2 * H:(s + 1) * n] for s in range(2)])

        w13_hi, w2_hi = split_views(sw_hi)
        w13_lo, w2_lo = split_views(sw_lo)

        psum = ctx.enter_context(nc.psum_tensor("psum", [P, 8, 512], fp32))

        edges_in, x_in, w_in = sem("edges_in"), sem("x_in"), sem("w_in")
        consts, pool_steps = sem("consts"), sem("pool_steps")
        w_hi_done, w_split = sem("w_hi_done"), sem("w_split")
        gate_t = sem("gate_t")
        onehot_ready, totals_ready, scan_done, prefix_ready = (
            sem("onehot_ready"), sem("totals_ready"), sem("scan_done"), sem("prefix_ready"))
        var_ready, sdev_ready = sem("var_ready"), sem("sdev_ready")
        xn_ready, xt_ready, xth_ready, xtl_ready, hw_ready, hw_evac = (
            sem("xn_ready"), sem("xt_ready"), sem("xth_ready"), sem("xtl_ready"), sem("hw_ready"), sem("hw_evac"))
        hw_stored = [sem(f"hw_stored{s}") for s in range(2)]
        sort_ready, sort_used, sorted_ready = (
            sem("sort_ready"), sem("sort_used"), sem("sorted_ready"))
        dve_rank, dve_ln, dve_block, dve_route, dve_tok = (
            sem("dve_rank"), sem("dve_ln"), sem("dve_block"), sem("dve_route"), sem("dve_tok"))
        staged = sem("staged")
        gathered = [sem(f"gathered{h}") for h in range(2)]
        ghi_ready, ring_freed, split_ready, agg_used, agg_ready, x1_done = (
            sem("ghi_ready"), sem("ring_freed"), sem("split_ready"), sem("agg_used"), sem("agg_ready"), sem("x1_done"))
        mv2_ready, sd2_ready, xn2_ready, xn2_stored = sem("mv2_ready"), sem("sd2_ready"), sem("xn2_ready"), sem("xn2_stored")
        t2_ready, x2h_ready, x2l_ready, h_ready, silu_ready, hs_ready = (
            sem("t2_ready"), sem("x2h_ready"), sem("x2l_ready"), sem("h_ready"), sem("silu_ready"), sem("hs_ready"))
        hT_ready, hTh_ready, hTl_ready, y_ready, shared_done = (
            sem("hT_ready"), sem("hTh_ready"), sem("hTl_ready"), sem("y_ready"), sem("shared_done"))
        top_ready, sig_ready, pairs_oh, rtot, rscan, rpre, texp_c, texp_t, tables = (
            sem("top_ready"), sem("sig_ready"), sem("pairs_oh"), sem("rtot"), sem("rscan"), sem("rpre"),
            sem("texp_c"), sem("texp_t"), sem("tables"))
        tsort_ready, tsort_used = sem("tsort_ready"), sem("tsort_used")
        w_loaded = [sem(f"w_loaded{s}") for s in range(2)]
        xg_in = [sem(f"xg_in{s}") for s in range(2)]
        w13h, w13l, w2h, w2l = sem("w13h"), sem("w13l"), sem("w2h"), sem("w2l")
        ext_ready, exh_ready, exl_ready, h13_ready, sil_ready, eh_ready = (
            sem("ext_ready"), sem("exh_ready"), sem("exl_ready"), sem("h13_ready"), sem("sil_ready"), sem("eh_ready"))
        eht_ready, ehth_ready, ehtl_ready, ey_ready, ey_evac = (
            sem("eht_ready"), sem("ehth_ready"), sem("ehtl_ready"), sem("ey_ready"), sem("ey_evac"))
        ys_stored = [sem(f"ys_stored{s}") for s in range(2)]
        ys_zeroed = sem("ys_zeroed")
        cstaged, held = sem("cstaged"), sem("held")
        yg_in = [sem(f"yg_in{s}") for s in range(HALF)]
        combined, out_stored, comb_steps = sem("combined"), sem("out_stored"), sem("comb_steps")

        def hold(engine):
            engine.sem_inc(held, 1)

        def mm3(pe, o, a_hi, a_lo, b_hi, b_lo, first, last):
            pe.matmul(o, a_hi, b_hi, start=first, stop=False)
            pe.matmul(o, a_lo, b_hi, start=False, stop=False)
            return pe.matmul(o, a_hi, b_lo, start=False, stop=last)

        def rows4(ap, k, n):
            return ap.rearrange("p (m n) -> p n m", n=n)[:, k, :]

        block = ctx.enter_context(nc.Block())

        @block.sync
        def _(sp):
            sp.dma_start(src_i, src.rearrange("(p k) -> p k", p=P)).then_inc(edges_in, 16)
            sp.dma_start(dst_i, dst.rearrange("(p k) -> p k", p=P)).then_inc(edges_in, 16)
            sp.dma_start(ew_f, edge_weight.rearrange("(p k) -> p k", p=P)).then_inc(edges_in, 16)
            sp.dma_start(acc[:], x.rearrange("(t p) d -> p t d", p=P)).then_inc(x_in, 16)
            for m, w in enumerate((gnn_w, sw1, sw3, sw2)):
                sp.dma_start(raw[:, m], w.rearrange("(p k) n -> p k n", p=P)).then_inc(w_in, 16)
            sp.dma_start(gate_f, gate_w).then_inc(w_in, 16)
            sp.dma_start(bias_f, gnn_bias.rearrange("(a d) -> a d", a=1)).then_inc(w_in, 16)
            sp.wait_ge(consts, 1)
            zero_row = zeros[:].bitcast(fp32)
            zero_part = 16
            for q in range(2 * MAX_TILES // zero_part):
                sp.dma_start(ys_dram.rearrange("(p r) (h n) -> p (r h) n", p=P, h=2)[:, zero_part * q:zero_part * (q + 1)],
                             zero_row.unsqueeze(1).to_broadcast([P, zero_part, D // 2])).then_inc(ys_zeroed, 16)
            with sp.Fori(0, TILES) as t:
                sp.wait_ge(xn2_ready, t + 1)
                sp.dma_start(xn_dram[bass.ds(t * P, P), :], xn[:, 0]).then_inc(xn2_stored, 16)
            sp.wait_ge(tables, 1)
            later = sp.value_load(groups[0:1, 0:1], min_val=1, max_val=MAX_TILES // 2 - 1)
            with sp.Fori(0, later + 1) as g:
                for s in range(2):
                    e = sp.value_load(texp_row[0:1, bass.ds(2 * g + s, 1)], min_val=0, max_val=EXPERTS - 1)
                    sp.wait_ge(w2l, 2 * g + s + 1)
                    for m, w in enumerate((w1, w3)):
                        sp.dma_start(w13_raw[s][:, m], w[bass.ds(e, 1)].rearrange("a (p k) n -> p (a k) n", p=P)
                                     ).then_inc(w_loaded[s], 16)
                    sp.dma_start(w2_raw[s], w2[bass.ds(e, 1)].rearrange("a (p k) n -> p (a k) n", p=P)
                                 ).then_inc(w_loaded[s], 16)
            with sp.Fori(0, TILES) as t:
                sp.wait_ge(combined, t + 1)
                sp.dma_start(out[bass.ds(t * P, P), :], acc[:, bass.ds(t, 1), :]).then_inc(out_stored, 16)
            sp.wait_ge(out_stored, 16 * TILES)

        @block.gpsimd
        def _(pool):
            st = Steps(pool, pool_steps)
            st.add(pool.memset(ident[:], 0.0))
            st.add(pool.memset(before_neg[:], -1.0))
            st.add(pool.iota(iota_i, [[1, CHUNKS]], base=0, channel_multiplier=0))
            st.add(pool.iota(tok_i[:], [[P, TILES]], base=0, channel_multiplier=1))
            st.wait()
            st.add(pool.affine_select(out=ident[:], in_=ident[:], compare_op=ALU.not_equal, fill=1.0,
                                      base=0, pattern=[[-1, P]], channel_multiplier=1))
            st.add(pool.affine_select(out=before_neg[:], in_=before_neg[:], compare_op=ALU.is_ge, fill=0.0,
                                      base=0, pattern=[[-1, P]], channel_multiplier=1))
            st.add(pool.tensor_copy(iota_f[:], iota_i))
            st.add(pool.tensor_copy(tok_f[:], tok_i[:]))
            st.add(pool.memset(ones_b[:], 1.0))
            st.add(pool.memset(one_f[:], 1.0))
            st.add(pool.memset(zeros[:], 0.0))
            st.add(pool.memset(eps_t[:], EPS))
            st.add(pool.memset(tok_sorted[:], 0))
            st.wait()
            pool.sem_inc(consts, 1)
            pool.wait_ge(sorted_ready, 1)
            for s in range(2):
                pool.wait_ge(hw_stored[s], 16 * (TILES // 2))
            with pool.Fori(0, CHUNKS // RING) as i:
                for h in range(2):
                    pool.wait_ge(ring_freed, RING * i + HALF * (h + 1))
                    pool.tensor_copy(stage[:, h], sdst[:, bass.ds(RING * i + HALF * h, HALF)]).then_inc(staged, 1)
                    pool.wait_ge(staged, 2 * i + h + 1)
                    hold(pool)
                    for r in range(HALF):
                        pool.indirect_dma_start(ring[:, HALF * h + r], None, hw_dram,
                                                bass.IndirectOffsetOnAxis(stage[:, h, r:r + 1], 0)
                                                ).then_inc(gathered[h], 16)
            pool.wait_ge(tables, 1)
            pool.wait_ge(xn2_stored, 16 * TILES)
            later = pool.value_load(groups[0:1, 0:1], min_val=1, max_val=MAX_TILES // 2 - 1)
            done = 2 * (CHUNKS // RING)
            with pool.Fori(0, later + 1) as g:
                for s in range(2):
                    pool.wait_ge(ext_ready, 2 * g + s + 1)
                    pool.tensor_copy(stage[:, s, 0:1], tok_sorted[:, bass.ds(2 * g + s, 1)]).then_inc(staged, 1)
                    pool.wait_ge(staged, 2 * g + (done + s + 1))
                    hold(pool)
                    pool.indirect_dma_start(hwb[:, s], None, xn_dram,
                                            bass.IndirectOffsetOnAxis(stage[:, s, 0:1], 0)).then_inc(xg_in[s], 16)
            for s in range(2):
                pool.wait_ge(ys_stored[s], 16 * later + 16)
            hold(pool)
            with pool.Fori(0, TILES * TOPK // HALF) as i:
                pool.wait_ge(combined, i * (HALF // TOPK))
                pool.tensor_copy(stage[:, 0], comb_idx[:].rearrange("p t k -> p (t k)")[:, bass.ds(i * HALF, HALF)]
                                 ).then_inc(cstaged, 1)
                pool.wait_ge(cstaged, i + 1)
                hold(pool)
                for r in range(HALF):
                    pool.indirect_dma_start(ring[:, r], None, ys_dram,
                                            bass.IndirectOffsetOnAxis(stage[:, 0, r:r + 1], 0)
                                            ).then_inc(yg_in[r], 16)

        @block.tensor
        def _(pe):
            pe.sem_inc(sort_used, 2)
            pe.sem_inc(agg_used, 2)
            pe.sem_inc(tsort_used, 2)
            pe.sem_inc(ext_ready, 2)
            pe.sem_inc(h13_ready, 2)
            pe.sem_inc(ey_ready, 2)
            pe.wait_ge(consts, 1)
            pe.wait_ge(onehot_ready, 1)
            for b in range(8):
                pe.matmul(psum[:, b], ones_b[:], onehot[:, 512 * b:512 * b + 512], start=True, stop=True
                          ).then_inc(totals_ready, 1)
            for b in range(8):
                pe.wait_ge(scan_done, b + 1)
                pe.matmul(psum[:, b], before_neg[:], onehot[:, 512 * b:512 * b + 512], start=True, stop=True
                          ).then_inc(prefix_ready, 1)
            pe.wait_ge(w_in, 96)
            pe.wait_ge(scan_done, 9)
            for k in range(KD):
                last = pe.transpose(psum[:, 4, EXPERTS * k:EXPERTS * (k + 1)], rows4(gate_f, k, KD),
                                    ident[0:EXPERTS, 0:EXPERTS])
            last.then_inc(gate_t, 1)
            pe.wait_ge(w_split, 1)
            with pe.Fori(0, TILES // 2) as i:
                for s in range(2):
                    pe.wait_ge(xn_ready, 2 * i + s + 1)
                    for k in range(KD):
                        last = pe.transpose(psum[:, 4 + s, P * k:P * (k + 1)], rows4(xn[:, s], k, KD), ident[:])
                    last.then_inc(xt_ready, 1)
                for s in range(2):
                    pe.wait_ge(xtl_ready, 2 * i + s + 1)
                    pe.wait_ge(hw_evac, 2 * i)
                    for k in range(KD):
                        last = mm3(pe, psum[:, 6 + s], xt_hi[:, s, k], xt_lo[:, s, k], gw_hi[:, k], gw_lo[:, k],
                                   k == 0, k == KD - 1)
                    last.then_inc(hw_ready, 1)
            for f in range(4):
                pe.matmul(psum[:, f, 0:CHUNKS], zeros_r[:, 0:P], zeros_r[:], start=True, stop=True)
            with pe.Fori(0, EC // 2) as i:
                for s in range(2):
                    pe.wait_ge(sort_ready, 2 * i + s + 1)
                    for f in range(4):
                        last = pe.matmul(psum[:, f, 0:CHUNKS], lane_oh[:, s, f], tile_oh[:, s], start=False, stop=True,
                                         skip_group_check=True)
                    last.then_inc(sort_used, 1)
            pe.wait_ge(sorted_ready, 1)
            with pe.Fori(0, TILES) as t:
                first = pe.value_load(pair_tab[0:1, bass.ds(t, 1)], min_val=0, max_val=PAIRS)
                end = pe.value_load(pair_tab[0:1, bass.ds(t + 1, 1)], min_val=0, max_val=PAIRS)
                pe.wait_ge(x1_done, t)
                pe.matmul(psum[:, 0], one_r[:], bias_hi[:], start=True, stop=True)
                with pe.Fori(first, end) as j:
                    for s in range(2):
                        pe.wait_ge(split_ready, 2 * j + (s + 1))
                        pe.matmul(psum[:, 0], row_oh[:, s], g_hi[:, s], start=False, stop=True, skip_group_check=True)
                        pe.matmul(psum[:, 0], row_oh[:, s], g_lo[:, s], start=False, stop=True, skip_group_check=True
                                  ).then_inc(agg_used, 1)
                pe.matmul(psum[:, 0], one_r[:], bias_lo[:], start=False, stop=True, skip_group_check=True
                          ).then_inc(agg_ready, 1)
                pe.wait_ge(xn2_ready, t + 1)
                for k in range(KD):
                    last = pe.transpose(psum[:, 1, P * k:P * (k + 1)], rows4(xn[:, 0], k, KD), ident[:])
                last.then_inc(t2_ready, 1)
                pe.wait_ge(x2l_ready, t + 1)
                pe.wait_ge(shared_done, t)
                for k in range(KD):
                    mm3(pe, psum[:, 2, 0:EXPERTS], xt_hi[:, 0, k], xt_lo[:, 0, k], gt_hi[:, k], gt_lo[:, k],
                        k == 0, k == KD - 1)
                for m in range(2):
                    for k in range(KD):
                        last = mm3(pe, psum[:, 3 + m], xt_hi[:, 0, k], xt_lo[:, 0, k], sw_hi[:, m, k], sw_lo[:, m, k],
                                   k == 0, k == KD - 1)
                last.then_inc(h_ready, 1)
                pe.wait_ge(hs_ready, t + 1)
                for k in range(KD):
                    last = pe.transpose(psum[:, 5, P * k:P * (k + 1)], rows4(hid[:, 1], k, KD), ident[:])
                last.then_inc(hT_ready, 1)
                pe.wait_ge(hTl_ready, t + 1)
                for k in range(KD):
                    last = mm3(pe, psum[:, 6], ht_hi[:, k], ht_lo[:, k], sw_hi[:, 2, k], sw_lo[:, 2, k],
                               k == 0, k == KD - 1)
                last.then_inc(y_ready, 1)
            pe.wait_ge(pairs_oh, 1)
            for b in range(2):
                last = pe.matmul(psum[:, b], ones_b[:], onehot[:, 512 * b:512 * b + 512], start=True, stop=True)
            last.then_inc(rtot, 1)
            for b in range(2):
                last = pe.matmul(psum[:, 2 + b], before_neg[:], onehot[:, 512 * b:512 * b + 512], start=True, stop=True)
            last.then_inc(rpre, 1)
            pe.wait_ge(texp_c, 1)
            pe.matmul(psum[0:1, 5, 0:P], texp_f[:, 1:2], ident[:], start=True, stop=True).then_inc(texp_t, 1)
            pe.matmul(psum[:, 4, 0:MAX_TILES], zeros_r[:, 0:P], zeros_r[:, 0:MAX_TILES], start=True, stop=True)
            with pe.Fori(0, TILES) as t:
                for k in range(TOPK):
                    pe.wait_ge(tsort_ready, 2 * t + k + 1)
                    pe.matmul(psum[:, 4, 0:MAX_TILES], lane_oh[:, k, 0], tile_oh[:, k, 0:MAX_TILES],
                              start=False, stop=True, skip_group_check=True).then_inc(tsort_used, 1)
            pe.wait_ge(tables, 1)
            later = pe.value_load(groups[0:1, 0:1], min_val=1, max_val=MAX_TILES // 2 - 1)

            def x_transpose(b, c):
                s = c % 2
                pe.wait_ge(xg_in[s], b * 8 + (c - s) * 8 + 16)
                for k in range(KD):
                    last = pe.transpose(psum[:, s, P * k:P * (k + 1)], rows4(hwb[:, s], k, KD), ident[:])
                last.then_inc(ext_ready, 1)

            def up(b, c):
                s = c % 2
                pe.wait_ge(exl_ready, b + (c + 1))
                pe.wait_ge(w13l, b + (c + 1))
                for k in range(KD):
                    last = mm3(pe, psum[:, 2 + s], xt_hi[:, s, k], xt_lo[:, s, k],
                               w13_hi[s].rearrange("p (m k n) -> p m k n", m=2, k=KD)[:, :, k],
                               w13_lo[s].rearrange("p (m k n) -> p m k n", m=2, k=KD)[:, :, k],
                               k == 0, k == KD - 1)
                last.then_inc(h13_ready, 1)

            def h_transpose(b, c):
                s = c % 2
                pe.wait_ge(eh_ready, b + (c + 1))
                for k in range(KH):
                    last = pe.transpose(psum[:, 4 + s, P * k:P * (k + 1)], rows4(hid[:, s, H:2 * H], k, KH), ident[:])
                last.then_inc(eht_ready, 1)

            def down(b, c):
                s = c % 2
                pe.wait_ge(ehtl_ready, b + (c + 1))
                pe.wait_ge(w2l, b + (c + 3))
                pe.wait_ge(ey_evac, b + (c - s))
                for k in range(KH):
                    last = mm3(pe, psum[:, 6 + s], ht_hi[:, 2 * s + k], ht_lo[:, 2 * s + k],
                               w2_hi[s].rearrange("p (k n) -> p k n", k=KH)[:, k],
                               w2_lo[s].rearrange("p (k n) -> p k n", k=KH)[:, k], k == 0, k == KH - 1)
                last.then_inc(ey_ready, 1)

            def step(b, c):
                x_transpose(b, c)
                h_transpose(b, c - 1)
                up(b, c)
                down(b, c - 1)

            x_transpose(0, 0)
            up(0, 0)
            with pe.Fori(0, later) as g:
                step(2 * g, 1)
                step(2 * g, 2)
            step(2 * later, 1)
            h_transpose(2 * later, 1)
            down(2 * later, 1)

        @block.scalar
        def _(act):
            act.wait_ge(w_in, 96)
            act.wait_ge(consts, 1)
            nc.scalar.copy(gw_hi[:], raw[:, 0]).then_inc(w_hi_done, 1)
            for m in range(3):
                nc.scalar.copy(sw_hi[:, m], raw[:, m + 1]).then_inc(w_hi_done, 1)
            nc.scalar.copy(bias_hi[:], bias_f).then_inc(w_hi_done, 1)
            nc.scalar.copy(one_r[:], one_f[:]).then_inc(w_hi_done, 1)
            nc.scalar.copy(zeros_r[:], zeros[:, 0:CHUNKS]).then_inc(w_hi_done, 1)
            act.wait_ge(gate_t, 1)
            nc.scalar.copy(gt_hi[:], psum[:, 4, 0:KD * EXPERTS].rearrange("p (k e) -> p k e", k=KD)
                           ).then_inc(w_hi_done, 1)
            act.wait_ge(var_ready, 1)
            nc.scalar.activation(sdev[:], mv[:, :, 1], ACT.Sqrt, bias=eps_t[:]).then_inc(sdev_ready, 1)
            with act.Fori(0, TILES // 2) as i:
                for s in range(2):
                    act.wait_ge(xt_ready, 2 * i + s + 1)
                    nc.scalar.copy(xt_hi[:, s], psum[:, 4 + s].rearrange("p (k n) -> p k n", k=KD)
                                   ).then_inc(xth_ready, 1)
                for s in range(2):
                    act.wait_ge(hw_ready, 2 * i + s + 1)
                    act.wait_ge(hw_stored[s], 16 * i)
                    nc.scalar.copy(hwb[:, s], psum[:, 6 + s]).then_inc(hw_evac, 1)
                    act.wait_ge(hw_evac, 2 * i + s + 1)
                    act.dma_start(hw_dram[bass.ds((2 * i + s) * P, P), :], hwb[:, s]).then_inc(hw_stored[s], 16)
            act.wait_ge(sorted_ready, 1)
            with act.Fori(0, TILES) as t:
                first = act.value_load(pair_tab[0:1, bass.ds(t, 1)], min_val=0, max_val=PAIRS)
                end = act.value_load(pair_tab[0:1, bass.ds(t + 1, 1)], min_val=0, max_val=PAIRS)
                with act.Fori(first, end) as j:
                    act.wait_ge(gathered[0], (j // HALF) * (16 * HALF) + 16 * HALF)
                    act.wait_ge(gathered[1], ((j + HALF // 2) // HALF) * (16 * HALF))
                    for s in range(2):
                        act.wait_ge(agg_used, 2 * j + (s + 1))
                        nc.scalar.activation(g_hi[:, s], ring[:, bass.ds((j % HALF) * 2 + s, 1), :], ACT.Copy,
                                             scale=sew[:, bass.ds(2 * j + s, 1)]).then_inc(ghi_ready, 1)
                act.wait_ge(mv2_ready, t + 1)
                nc.scalar.activation(sdev[:, 0:1], mv[:, 0, 1:2], ACT.Sqrt, bias=eps_t[:]).then_inc(sd2_ready, 1)
                act.wait_ge(t2_ready, t + 1)
                nc.scalar.copy(xt_hi[:, 0], psum[:, 1].rearrange("p (k n) -> p k n", k=KD)).then_inc(x2h_ready, 1)
                act.wait_ge(h_ready, t + 1)
                nc.scalar.copy(logits[:, bass.ds(t, 1), :], psum[:, 2, 0:EXPERTS])
                nc.scalar.activation(hid[:, 0], psum[:, 3], ACT.Silu).then_inc(silu_ready, 1)
                act.wait_ge(hT_ready, t + 1)
                nc.scalar.copy(ht_hi, psum[:, 5].rearrange("p (k n) -> p k n", k=KD)).then_inc(hTh_ready, 1)
            act.wait_ge(top_ready, 1)
            nc.scalar.activation(r_small[:, 0], top8[:, :, 0:TOPK].rearrange("p t k -> p k t"), ACT.Sigmoid
                                 ).then_inc(sig_ready, 1)
            act.wait_ge(tables, 1)
            later = act.value_load(groups[0:1, 0:1], min_val=1, max_val=MAX_TILES // 2 - 1)

            def split13(b, c):
                s = c % 2
                act.wait_ge(w_loaded[s], b * 24 + (c - s) * 24 + 48)
                act.wait_ge(h13_ready, b + (c + 1))
                nc.scalar.copy(w13_hi[s], w_raw[s][:, 0:KD * 2 * H]).then_inc(w13h, 1)

            def split2(b, c):
                s = c % 2
                act.wait_ge(ey_ready, b + (c + 1))
                nc.scalar.copy(w2_hi[s], w_raw[s][:, KD * 2 * H:]).then_inc(w2h, 1)

            def x_high(b, c):
                s = c % 2
                act.wait_ge(ext_ready, b + (c + 3))
                nc.scalar.copy(xt_hi[:, s], psum[:, s].rearrange("p (k n) -> p k n", k=KD)).then_inc(exh_ready, 1)

            def h_high(b, c):
                s = c % 2
                act.wait_ge(eht_ready, b + (c + 1))
                nc.scalar.copy(ht_hi[:, 2 * s:2 * s + 2], psum[:, 4 + s, 0:H].rearrange("p (k n) -> p k n", k=KH)
                               ).then_inc(ehth_ready, 1)

            def silu(b, c):
                s = c % 2
                act.wait_ge(h13_ready, b + (c + 3))
                nc.scalar.activation(hid[:, s, 0:H], psum[:, 2 + s, 0:H], ACT.Silu).then_inc(sil_ready, 1)

            def store(b, c):
                s = c % 2
                act.wait_ge(ey_ready, b + (c + 3))
                act.wait_ge(ys_stored[s], b * 8 + (c - s) * 8)
                nc.scalar.copy(xn[:, s], psum[:, 6 + s]).then_inc(ey_evac, 1)
                act.wait_ge(ey_evac, b + (c + 1))
                act.dma_start(ys_dram[bass.ds(b * P + c * P, P), :], xn[:, s]).then_inc(ys_stored[s], 16)

            def step(b, c, more=True):
                x_high(b, c)
                h_high(b, c - 1)
                if more:
                    split13(b, c + 1)
                silu(b, c)
                if more:
                    split2(b, c + 1)
                store(b, c - 1)

            act.wait_ge(ys_zeroed, 16 * (2 * MAX_TILES // 16))
            split13(0, 0)
            split2(0, 0)
            x_high(0, 0)
            split13(0, 1)
            silu(0, 0)
            split2(0, 1)
            with act.Fori(0, later) as g:
                step(2 * g, 1)
                step(2 * g, 2)
            step(2 * later, 1, more=False)
            h_high(2 * later, 1)
            store(2 * later, 1)

        @block.vector
        def _(v):
            v.sem_inc(ring_freed, RING)
            v.sem_inc(w2l, 2)
            st = Steps(v, dve_rank)
            v.wait_ge(edges_in, 48)
            st.add(v.tensor_scalar(block_i, src_i, BLOCK_SHIFT, None, ALU.logical_shift_right))
            st.add(v.tensor_scalar(lane_i, src_i, P - 1, None, ALU.bitwise_and))
            st.add(v.tensor_copy(ew_r, ew_f))
            st.add(v.tensor_copy(rec[:, 0], dst_i))
            st.wait()
            st.add(v.tensor_copy(block_f, block_i))
            st.add(v.tensor_copy(rec[:, 1], lane_i))
            st.add(v.tensor_copy(rec[:, 2], ew_r.bitcast(fp32)))
            st.add(v.tensor_tensor(rec[:, 3], ew_f, ew_r.bitcast(fp32), ALU.subtract))
            st.wait()
            oh3 = onehot[:].rearrange("p (b k) -> p b k", b=TILES)
            for b in range(TILES):
                last = v.tensor_scalar(oh3[:, b], block_f, float(b), None, ALU.is_equal)
            last.then_inc(onehot_ready, 1)
            v.wait_ge(consts, 1)
            for b in range(8):
                v.wait_ge(totals_ready, b + 1)
                v.tensor_tensor_scan(scan[:, 512 * b:512 * b + 512], psum[:, b], zeros[:],
                                     0.0 if b == 0 else scan[:, 512 * b - 1:512 * b], ALU.add, ALU.add
                                     ).then_inc(scan_done, 1)
                v.wait_ge(scan_done, b + 1)
            scan3 = scan[:].rearrange("p (b k) -> p b k", b=TILES)
            last_count = scan3[:, :, EC - 1]
            cnt, n_pairs, p_end, p_start, corr, tmp = (ends[:, j] for j in range(6))
            st.add(v.tensor_copy(cnt[:, 0:1], last_count[:, 0:1]))
            st.add(v.tensor_tensor(cnt[:, 1:], last_count[:, 1:], last_count[:, 0:TILES - 1], ALU.subtract))
            st.wait()
            st(v.tensor_scalar(tmp, cnt, float(PAIR * P - 1), None, ALU.add))
            st(v.tensor_copy(ends_i[:], tmp))
            st(v.tensor_scalar(ends_i[:], ends_i[:], PAIR_SHIFT, None, ALU.logical_shift_right))
            st(v.tensor_copy(n_pairs, ends_i[:]))
            st(v.tensor_scalar(n_pairs, n_pairs, 1.0, None, ALU.max))
            st(v.tensor_tensor_scan(p_end, n_pairs, zeros[:, 0:TILES], 0.0, ALU.add, ALU.add))
            st(v.tensor_tensor(p_start, p_end, n_pairs, ALU.subtract))
            st.add(v.tensor_copy(pair_tab[:, 0:TILES], p_start))
            st.add(v.memset(pair_tab[:, TILES:], PAIRS))
            st(v.tensor_tensor(corr, last_count, cnt, ALU.subtract))
            st(v.scalar_tensor_tensor(corr, p_start, float(PAIR * P), corr, ALU.mult, ALU.subtract))
            work3 = work[:].rearrange("p (b k) -> p b k", b=TILES)
            for b in range(TILES):
                v.wait_ge(prefix_ready, b // 2 + 1)
                st.add(v.scalar_tensor_tensor(work3[:, b], scan3[:, b], corr[:, b:b + 1],
                                              psum[:, b // 2, EC * (b % 2):EC * (b % 2 + 1)], ALU.add, ALU.add))
            st.wait()
            v.sem_inc(scan_done, 1)
            st(v.tensor_tensor(work[:], work[:], onehot[:], ALU.mult))
            st(v.tensor_reduce(pos_f, work3.rearrange("p b k -> p k b"), AX.X, ALU.add))
            st(v.tensor_copy(pos_i, pos_f))
            st.add(v.tensor_scalar(block_i, pos_i, BLOCK_SHIFT, None, ALU.logical_shift_right))
            st.add(v.tensor_scalar(lane_i, pos_i, P - 1, None, ALU.bitwise_and))
            st.wait()
            st.add(v.tensor_copy(slot_tile[:], block_i))
            st.add(v.tensor_copy(slot_lane[:], lane_i))
            st.wait()
            v.wait_ge(w_in, 96)
            v.wait_ge(w_hi_done, 4)
            v.tensor_tensor(gw_lo[:], raw[:, 0], gw_hi[:].bitcast(fp32), ALU.subtract)
            for m in range(3):
                v.tensor_tensor(sw_lo[:, m], raw[:, m + 1], sw_hi[:, m].bitcast(fp32), ALU.subtract)
            v.wait_ge(w_hi_done, 8)
            v.tensor_tensor(bias_lo[:], bias_f, bias_hi[:].bitcast(fp32), ALU.subtract)
            v.tensor_tensor(gt_lo[:], psum[:, 4, 0:KD * EXPERTS].rearrange("p (k e) -> p k e", k=KD),
                            gt_hi[:].bitcast(fp32), ALU.subtract).then_inc(w_split, 1)
            v.wait_ge(x_in, 16)
            sl = Steps(v, dve_ln)
            for t in range(TILES):
                sl.add(v.bn_stats(stats[:, t], acc[:, t]))
            sl.wait()
            for t in range(TILES):
                last = v.bn_aggr(mv[:, t], stats[:, t])
            last.then_inc(var_ready, 1)
            v.wait_ge(sdev_ready, 1)
            sl(v.reciprocal(rstd[:], sdev[:]))
            with v.Fori(0, TILES // 2) as i:
                for s in range(2):
                    v.wait_ge(xt_ready, 2 * i)
                    n = 2 * i + s
                    v.tensor_scalar(xn[:, s], acc[:, bass.ds(n, 1), :], mv[:, bass.ds(n, 1), 0:1].rearrange("p a b -> p (a b)"),
                                    rstd[:, bass.ds(n, 1)], ALU.subtract, ALU.mult).then_inc(xn_ready, 1)
                for s in range(2):
                    v.wait_ge(xth_ready, 2 * i + s + 1)
                    v.tensor_tensor(xt_lo[:, s], psum[:, 4 + s].rearrange("p (k n) -> p k n", k=KD),
                                    xt_hi[:, s].bitcast(fp32), ALU.subtract).then_inc(xtl_ready, 1)
            v.wait_ge(hw_ready, TILES)
            with v.Fori(0, EC // 2) as i:
                for s in range(2):
                    c = 2 * i + s
                    v.wait_ge(sort_used, 2 * i + s + 1)
                    for f in range(4):
                        v.tensor_scalar(lane_oh[:, s, f], iota_f[:, 0:P], slot_lane[:, bass.ds(c, 1)],
                                        rec[:, f, bass.ds(c, 1)], ALU.is_equal, ALU.mult)
                    v.tensor_scalar(tile_oh[:, s], iota_f[:], slot_tile[:, bass.ds(c, 1)], None, ALU.is_equal
                                    ).then_inc(sort_ready, 1)
            v.wait_ge(sort_used, EC + 2)
            v.tensor_copy(sdst, psum[:, 0, 0:CHUNKS])
            v.tensor_copy(slane, psum[:, 1, 0:CHUNKS])
            sl(v.tensor_copy(sew, psum[:, 2, 0:CHUNKS]))
            sl(v.tensor_tensor(sew, sew, psum[:, 3, 0:CHUNKS], ALU.add))
            v.sem_inc(sorted_ready, 1)
            sk = Steps(v, dve_block)
            with v.Fori(0, TILES) as t:
                sk.enter(t, 2)
                first = v.value_load(pair_tab[0:1, bass.ds(t, 1)], min_val=0, max_val=PAIRS)
                end = v.value_load(pair_tab[0:1, bass.ds(t + 1, 1)], min_val=0, max_val=PAIRS)
                with v.Fori(first, end) as j:
                    for s in range(2):
                        v.wait_ge(ghi_ready, 2 * j + (s + 1))
                        v.scalar_tensor_tensor(g_lo[:, s], ring[:, bass.ds((j % HALF) * 2 + s, 1), :].rearrange("p a n -> p (a n)"),
                                               sew[:, bass.ds(2 * j + s, 1)], g_hi[:, s].bitcast(fp32),
                                               ALU.mult, ALU.subtract).then_inc(ring_freed, 1)
                        v.tensor_scalar(row_oh[:, s], iota_f[:, 0:P], slane[:, bass.ds(2 * j + s, 1)], None,
                                        ALU.is_equal).then_inc(split_ready, 1)
                v.wait_ge(agg_ready, t + 1)
                acc_t = acc[:, bass.ds(t, 1), :].rearrange("p a n -> p (a n)")
                v.scalar_tensor_tensor(acc_t, psum[:, 0], 0.0, acc_t, ALU.max, ALU.add).then_inc(x1_done, 1)
                v.wait_ge(x1_done, t + 1)
                hold(v)
                sk(v.bn_stats(stats[:, 0], acc_t))
                hold(v)
                v.bn_aggr(mv[:, 0], stats[:, 0]).then_inc(mv2_ready, 1)
                v.wait_ge(mv2_ready, t + 1)
                v.wait_ge(sd2_ready, t + 1)
                sk(v.reciprocal(rstd[:, 0:1], sdev[:, 0:1]))
                v.wait_ge(xn2_stored, 16 * t)
                v.tensor_scalar(xn[:, 0], acc_t, mv[:, 0, 0:1], rstd[:, 0:1], ALU.subtract, ALU.mult
                                ).then_inc(xn2_ready, 1)
                v.wait_ge(x2h_ready, t + 1)
                v.tensor_tensor(xt_lo[:, 0], psum[:, 1].rearrange("p (k n) -> p k n", k=KD),
                                xt_hi[:, 0].bitcast(fp32), ALU.subtract).then_inc(x2l_ready, 1)
                v.wait_ge(silu_ready, t + 1)
                v.tensor_tensor(hid[:, 1], hid[:, 0], psum[:, 4], ALU.mult).then_inc(hs_ready, 1)
                v.wait_ge(hTh_ready, t + 1)
                v.tensor_tensor(ht_lo, psum[:, 5].rearrange("p (k n) -> p k n", k=KD),
                                ht_hi.bitcast(fp32), ALU.subtract).then_inc(hTl_ready, 1)
                v.wait_ge(y_ready, t + 1)
                v.tensor_tensor(acc_t, acc_t, psum[:, 6], ALU.add).then_inc(shared_done, 1)
                sk.leave(TILES)
            sr = Steps(v, dve_route)
            for t in range(TILES):
                sr.add(v.max(top8[:, t], logits[:, t]))
            sr.wait()
            v.sem_inc(top_ready, 1)
            for t in range(TILES):
                sr.add(v.max_index(idx8[:, t], top8[:, t], logits[:, t]))
            sr.wait()
            score, exp_f, rank, first_tile, valid, slot_c, slot_s, lane_f, tile_f, gate = (
                r_small[:, j] for j in range(10))
            oh_k = [work[:, 1024 * k:1024 * (k + 1)].rearrange("p (e t) -> p e t", t=TILES) for k in range(TOPK)]
            prod = work[:, 2048:3072].rearrange("p (e t) -> p e t", t=TILES)
            ranks = work[:, 3072:4096].rearrange("p (e t) -> p e t", t=TILES)
            oh_sum = onehot[:, 0:EXPERTS * TILES].rearrange("p (e t) -> p e t", t=TILES)
            big = [P, EXPERTS, TILES]
            sr(v.tensor_copy(exp_f, idx8[:, :, 0:TOPK].rearrange("p t k -> p k t")))
            for k in range(TOPK):
                sr.add(v.tensor_tensor(oh_k[k], exp_f[:, k].unsqueeze(1).to_broadcast(big),
                                       iota_f[:, 0:EXPERTS].unsqueeze(2).to_broadcast(big), ALU.is_equal))
            sr.wait()
            v.tensor_tensor(oh_sum, oh_k[0], oh_k[1], ALU.add).then_inc(pairs_oh, 1)
            v.wait_ge(sig_ready, 1)
            sr(v.tensor_tensor(gate[:, 0], score[:, 0], score[:, 1], ALU.add))
            sr(v.tensor_scalar(gate[:, 0], gate[:, 0], 1e-20, None, ALU.add))
            sr(v.reciprocal(gate[:, 1], gate[:, 0]))
            sr(v.tensor_tensor(gate[:, 0], score[:, 0], gate[:, 1], ALU.mult))
            sr(v.tensor_tensor(gate[:, 1], score[:, 1], gate[:, 1], ALU.mult))
            sr(v.tensor_scalar(gate, gate, ROUTE_SCALE, None, ALU.mult))
            v.wait_ge(rtot, 1)
            for b in range(2):
                sr(v.tensor_tensor_scan(scan[:, 512 * b:512 * b + 512], psum[:, b], zeros[:],
                                        0.0 if b == 0 else scan[:, 511:512], ALU.add, ALU.add))
            rscan3 = scan[:, 0:1024].rearrange("p (e t) -> p e t", t=TILES)
            e_end = rscan3[:, :, TILES - 1]
            e_cnt, e_start, e_tiles, t_end, t_start, e_tmp = (x_small[:, j] for j in range(6))
            sr.add(v.tensor_copy(e_cnt[:, 0:1], e_end[:, 0:1]))
            sr(v.tensor_tensor(e_cnt[:, 1:], e_end[:, 1:], e_end[:, 0:EXPERTS - 1], ALU.subtract))
            sr.add(v.tensor_tensor(e_start, e_end, e_cnt, ALU.subtract))
            sr(v.tensor_scalar(e_tmp, e_cnt, float(CAP), float(P - 1), ALU.min, ALU.add))
            sr(v.tensor_copy(x_int, e_tmp))
            sr(v.tensor_scalar(x_int, x_int, BLOCK_SHIFT, None, ALU.logical_shift_right))
            sr(v.tensor_copy(e_tiles, x_int))
            sr(v.tensor_tensor_scan(t_end, e_tiles, zeros[:, 0:EXPERTS], 0.0, ALU.add, ALU.add))
            sr.add(v.tensor_tensor(t_start, t_end, e_tiles, ALU.subtract))
            sr(v.tensor_scalar(x_small[:, 6], t_end, tok_f[:, 0:1], None, ALU.is_le))
            sr(v.tensor_reduce(texp_f[:, 0:1], x_small[:, 6], AX.X, ALU.add))
            v.tensor_scalar(texp_f[:, 1:2], texp_f[:, 0:1], float(EXPERTS - 1), None, ALU.min).then_inc(texp_c, 1)
            sr(v.tensor_scalar(x_small[:, 7, 0:1], t_end[:, EXPERTS - 1:EXPERTS], 1.0, None, ALU.add))
            sr(v.tensor_copy(x_int[:, 0:1], x_small[:, 7, 0:1]))
            sr(v.tensor_scalar(x_int[:, 0:1], x_int[:, 0:1], 1, None, ALU.logical_shift_right))
            sr(v.tensor_copy(x_small[:, 7, 0:1], x_int[:, 0:1]))
            sr(v.tensor_scalar(groups[:], x_small[:, 7, 0:1], -1.0, 1.0, ALU.add, ALU.max))
            v.wait_ge(rpre, 1)
            sr(v.tensor_tensor(ranks, rscan3, psum[:, 2:4].rearrange("p b (e t) -> p (b e) t", t=TILES), ALU.add))
            sr(v.tensor_tensor(ranks, ranks, e_start.unsqueeze(2).to_broadcast(big), ALU.subtract))
            for k in range(TOPK):
                sr(v.tensor_tensor(prod, oh_k[k], ranks, ALU.mult))
                sr(v.tensor_reduce(rank[:, k], prod.rearrange("p e t -> p t e"), AX.X, ALU.add))
                sr(v.tensor_tensor(prod, oh_k[k], t_start.unsqueeze(2).to_broadcast(big), ALU.mult))
                sr(v.tensor_reduce(first_tile[:, k], prod.rearrange("p e t -> p t e"), AX.X, ALU.add))
            sr(v.tensor_scalar(valid, rank, float(CAP), None, ALU.is_lt))
            sr(v.scalar_tensor_tensor(slot_c, first_tile, float(P), rank, ALU.mult, ALU.add))
            sr(v.tensor_tensor(slot_c, slot_c, valid, ALU.mult))
            sr.add(v.tensor_tensor(gate, gate, valid, ALU.mult))
            sr.add(v.tensor_copy(comb_idx[:].rearrange("p t k -> p k t"), slot_c))
            sr(v.tensor_scalar(slot_s, valid, float(-NOWHERE * P), float(NOWHERE * P), ALU.mult, ALU.add))
            sr(v.tensor_tensor(slot_s, slot_s, slot_c, ALU.add))
            sr(v.tensor_copy(r_int[:, 0], slot_s))
            sr.add(v.tensor_scalar(r_int[:, 1], r_int[:, 0], P - 1, None, ALU.bitwise_and))
            sr(v.tensor_scalar(r_int[:, 2], r_int[:, 0], BLOCK_SHIFT, None, ALU.logical_shift_right))
            sr.add(v.tensor_copy(lane_f, r_int[:, 1]))
            sr(v.tensor_copy(tile_f, r_int[:, 2]))
            v.wait_ge(texp_t, 1)
            sr(v.tensor_copy(texp_row[:], psum[0:1, 5, 0:P]))
            with v.Fori(0, TILES) as t:
                for k in range(TOPK):
                    v.wait_ge(tsort_used, 2 * t + k + 1)
                    v.tensor_scalar(lane_oh[:, k, 0], iota_f[:, 0:P], lane_f[:, k, bass.ds(t, 1)],
                                    tok_f[:, bass.ds(t, 1)], ALU.is_equal, ALU.mult)
                    v.tensor_scalar(tile_oh[:, k, 0:MAX_TILES], iota_f[:, 0:MAX_TILES], tile_f[:, k, bass.ds(t, 1)],
                                    None, ALU.is_equal).then_inc(tsort_ready, 1)
            v.wait_ge(tsort_used, TILES * TOPK + 2)
            sr(v.tensor_copy(tok_sorted[:, 0:MAX_TILES], psum[:, 4, 0:MAX_TILES]))
            v.sem_inc(tables, 1)
            later = v.value_load(groups[0:1, 0:1], min_val=1, max_val=MAX_TILES // 2 - 1)

            def split13(b, c):
                s = c % 2
                v.wait_ge(w13h, b + (c + 1))
                v.tensor_tensor(w13_lo[s], w_raw[s][:, 0:KD * 2 * H], w13_hi[s].bitcast(fp32), ALU.subtract
                                ).then_inc(w13l, 1)

            def split2(b, c):
                s = c % 2
                v.wait_ge(w2h, b + (c + 1))
                v.tensor_tensor(w2_lo[s], w_raw[s][:, KD * 2 * H:], w2_hi[s].bitcast(fp32), ALU.subtract
                                ).then_inc(w2l, 1)

            def x_low(b, c):
                s = c % 2
                v.wait_ge(exh_ready, b + (c + 1))
                v.tensor_tensor(xt_lo[:, s], psum[:, s].rearrange("p (k n) -> p k n", k=KD),
                                xt_hi[:, s].bitcast(fp32), ALU.subtract).then_inc(exl_ready, 1)

            def h_low(b, c):
                s = c % 2
                v.wait_ge(ehth_ready, b + (c + 1))
                v.tensor_tensor(ht_lo[:, 2 * s:2 * s + 2], psum[:, 4 + s, 0:H].rearrange("p (k n) -> p k n", k=KH),
                                ht_hi[:, 2 * s:2 * s + 2].bitcast(fp32), ALU.subtract).then_inc(ehtl_ready, 1)

            def gated(b, c):
                s = c % 2
                v.wait_ge(sil_ready, b + (c + 1))
                v.tensor_tensor(hid[:, s, H:2 * H], hid[:, s, 0:H], psum[:, 2 + s, H:2 * H], ALU.mult
                                ).then_inc(eh_ready, 1)

            def step(b, c, more=True):
                x_low(b, c)
                h_low(b, c - 1)
                if more:
                    split13(b, c + 1)
                gated(b, c)
                if more:
                    split2(b, c + 1)

            split13(0, 0)
            split2(0, 0)
            x_low(0, 0)
            split13(0, 1)
            gated(0, 0)
            split2(0, 1)
            with v.Fori(0, later) as g:
                step(2 * g, 1)
                step(2 * g, 2)
            step(2 * later, 1, more=False)
            h_low(2 * later, 1)
            per = HALF // TOPK
            with v.Fori(0, TILES // per) as i:
                for j in range(per):
                    t = per * i + j
                    acc_t = acc[:, bass.ds(t, 1), :].rearrange("p a n -> p (a n)")
                    v.wait_ge(yg_in[2 * j], 16 * i + 16)
                    v.scalar_tensor_tensor(acc_t, ring[:, 2 * j], gate[:, 0, bass.ds(t, 1)], acc_t, ALU.mult, ALU.add
                                           ).then_inc(comb_steps, 1)
                    v.wait_ge(comb_steps, per * i + j + 1)
                    v.wait_ge(yg_in[2 * j + 1], 16 * i + 16)
                    v.scalar_tensor_tensor(acc_t, ring[:, 2 * j + 1], gate[:, 1, bass.ds(t, 1)], acc_t,
                                           ALU.mult, ALU.add).then_inc(combined, 1)


_INS = ['x', 'src', 'dst', 'edge_weight', 'L0_gnn_W', 'L0_gnn_bias', 'L0_ffn_gate_w', 'L0_ffn_w1', 'L0_ffn_w3',
        'L0_ffn_w2', 'L0_ffn_sw1', 'L0_ffn_sw3', 'L0_ffn_sw2']
_OUTS = [((N, D), 'float32')]


def kernel(**inputs):
    import numpy as _np
    import concourse.bacc as _bacc
    from concourse.bass_utils import run_bass_kernel_spmd as _run

    nc = _bacc.Bacc("TRN2", target_bir_lowering=False, num_devices=1)
    arrays, args = {}, []
    for name in _INS:
        a = _np.ascontiguousarray(inputs[name])
        arrays[f"in_{name}_dram"] = a
        args.append(nc.dram_tensor(f"in_{name}_dram", a.shape, mybir.dt.from_np(a.dtype), kind="ExternalInput").ap())
    for i, (shape, dtype) in enumerate(_OUTS):
        dt = mybir.dt.from_np(_np.dtype(dtype))
        args.append(nc.dram_tensor(f"out_{i}_dram", shape, dt, kind="ExternalOutput").ap())
    build_program(nc, *args)
    r = _run(nc, [arrays], core_ids=[0])
    got = tuple(r.results[0][f"out_{i}_dram"] for i in range(len(_OUTS)))
    return got[0]
```

```python
import concourse.bass as bass
from concourse import mybir
from contextlib import ExitStack

fp32 = mybir.dt.float32
f32r = mybir.dt.float32r
bf16 = mybir.dt.bfloat16
i32 = mybir.dt.int32
u32 = mybir.dt.uint32
ALU = mybir.AluOpType
ACT = mybir.ActivationFunctionType
AX = mybir.AxisListType

P = 128
N, D = 2048, 512
E = 32768
EXPERTS, TOPK, H = 64, 2, 256
CAP = 1024
ROUTE_SCALE = 2.5
EPS = 1e-5
TILES = N // P
KD = D // P
KH = H // P
EC = E // P
QUAD = 4
QUADS = E // (QUAD * P) + TILES
CHUNKS = QUAD * QUADS
RING = 16
HALF = RING // 2
QUADS_RING = RING // QUAD
NORM_STEPS = 14
DRAIN = 4
BLOCK_SHIFT = 7
QUAD_SHIFT = 9
ROUND_SHIFT = 2
RSQRT_GUESS = 0x5f3759df
MAX_TILES = EXPERTS + N * TOPK // P
NOWHERE = 127
YROWS = MAX_TILES * P


class Steps:

    def __init__(self, engine, sem):
        self.engine, self.sem, self.base, self.n = engine, sem, 0, 0

    def add(self, instruction):
        instruction.then_inc(self.sem, 1)
        self.n += 1

    def wait(self):
        self.engine.wait_ge(self.sem, self.base + self.n)

    def __call__(self, instruction):
        self.add(instruction)
        self.wait()

    def enter(self, i, per):
        self.before, self.per = self.base + self.n, per
        self.base, self.n = self.before + i * per, 0

    def leave(self, times):
        assert self.n == self.per, (self.n, self.per)
        self.base, self.n = self.before + times * self.per, 0


def build_program(nc, x, src, dst, edge_weight, gnn_w, gnn_bias, gate_w, w1, w3, w2, sw1, sw3, sw2, out):
    ctx = ExitStack()
    with ctx:
        def sb(name, shape, dt):
            return ctx.enter_context(nc.sbuf_tensor(name, shape, dt))

        def sem(name):
            return ctx.enter_context(nc.semaphore(name))

        hw_dram = nc.dram_tensor("hw_dram", [N, D], fp32).ap()
        xn_dram = nc.dram_tensor("xn_dram", [N, D], fp32).ap()
        ys_dram = nc.dram_tensor("ys_dram", [YROWS, D], fp32).ap()

        acc = sb("acc", [P, TILES, D], fp32)
        raw = sb("raw", [P, 4, KD, D], fp32)
        ring = raw[:].rearrange("p a k n -> p (a k) n")
        sw_hi = sb("sw_hi", [P, 3, KD, D], f32r)
        sw_lo = sb("sw_lo", [P, 3, KD, D], f32r)
        gw_hi = sb("gw_hi", [P, KD, D], f32r)
        gw_lo = sb("gw_lo", [P, KD, D], f32r)
        scan = sb("scan", [P, TILES * EC], fp32)
        work = sb("work", [P, TILES * EC], fp32)
        onehot = sb("onehot", [P, TILES * EC], bf16)
        rec = sb("rec", [P, 4, EC], fp32)
        slot_tile = sb("slot_tile", [P, EC], fp32)
        slot_lane = sb("slot_lane", [P, EC], fp32)
        ends = sb("ends", [P, 6, TILES], fp32)
        ends_i = sb("ends_i", [P, TILES], i32)
        quad_tab = sb("quad_tab", [P, TILES + 1], i32)
        rounds = sb("rounds", [P, 1], i32)
        row_oh = sb("row_oh", [P, QUAD, P], f32r)
        scratch = sb("scratch", [P, 8, EC], fp32)
        src_i, dst_i, block_i, lane_i, pos_i = (scratch[:, j].bitcast(i32) for j in range(5))
        ew_f, block_f, pos_f = (scratch[:, j] for j in range(5, 8))
        rows2 = scratch[:].rearrange("p (a s b) k -> p a s (b k)", a=2, s=2)
        hwb, xn = rows2[:, 0], rows2[:, 1]
        tok_sorted = rec[:, 0, 0:MAX_TILES].bitcast(u32)
        texp_row = rec[0:1, 1, 0:P].bitcast(i32)
        sdst = scan[:, 1024:1024 + CHUNKS].bitcast(u32)
        slane = scan[:, 1024 + CHUNKS:1024 + 2 * CHUNKS]
        sew = scan[:, 1024 + 2 * CHUNKS:1024 + 3 * CHUNKS]
        logits = scan[:, 2048:2048 + TILES * EXPERTS].rearrange("p (t e) -> p t e", t=TILES)
        iota_i = scan[:, 0:CHUNKS].bitcast(i32)
        gw_hi_flat, gw_lo_flat = (t[:].rearrange("p k n -> p (k n)") for t in (gw_hi, gw_lo))
        lane_oh = gw_hi_flat.rearrange("p (s c f n) -> p s c f n", s=2, c=2, f=4)
        tile_oh = gw_lo_flat[:, 0:4 * CHUNKS].rearrange("p (s c n) -> p s c n", s=2, c=2)
        g_hi, g_lo = gw_hi, gw_lo
        ht_hi, ht_lo = gw_hi, gw_lo
        route = ring[:, HALF:RING].rearrange("p r n -> p (r n)")
        top8 = route[:, 0:128].rearrange("p (t j) -> p t j", t=TILES)
        idx8 = route[:, 128:256].bitcast(u32).rearrange("p (t j) -> p t j", t=TILES)
        r_small = route[:, 256:576].rearrange("p (j k t) -> p j k t", j=10, k=TOPK)
        r_int = route[:, 576:672].bitcast(i32).rearrange("p (j k t) -> p j k t", j=3, k=TOPK)
        x_small = route[:, 1024:1536].rearrange("p (j e) -> p j e", j=8)
        x_int = route[:, 1536:1600].bitcast(i32)
        stage = sb("stage", [P, RING], u32)
        bias_hi = sb("bias_hi", [1, D], f32r)
        bias_lo = sb("bias_lo", [1, D], f32r)
        gt_hi = sb("gt_hi", [P, KD, EXPERTS], f32r)
        gt_lo = sb("gt_lo", [P, KD, EXPERTS], f32r)
        xt_hi = sb("xt_hi", [P, 2, KD, P], f32r)
        ew_r = xt_hi[:, 0, 0:EC // P, :].rearrange("p k n -> p (k n)")
        xt_lo = sb("xt_lo", [P, 2, KD, P], f32r)
        sht_hi, sht_lo = xt_hi[:, 1], xt_lo[:, 1]
        hid = sb("hid", [P, 2, D], fp32)
        lane_plain = hid[:, 0].rearrange("p (s c n) -> p s c n", s=2, c=2)
        gate_f = hid[0:EXPERTS, 0]
        bias_f = hid[0:1, 1]
        stats = sb("stats", [P, TILES, 6], fp32)
        mv = sb("mv", [P, TILES, 2], fp32)
        rstd = sb("rstd", [P, TILES], fp32)
        newton = sb("newton", [P, 4, TILES], fp32)
        comb_idx = sb("comb_idx", [P, TILES, TOPK], u32)
        texp_f = sb("texp_f", [P, 2], fp32)
        groups = sb("groups", [P, 1], i32)
        ident = sb("ident", [P, P], fp32)
        before_neg = sb("before_neg", [P, P], bf16)
        ones_b = sb("ones_b", [P, P], bf16)
        one_r = sb("one_r", [1, P], f32r)
        iota_f = sb("iota_f", [P, CHUNKS], fp32)
        tok_i = sb("tok_i", [P, TILES], i32)
        tok_f = sb("tok_f", [P, TILES], fp32)
        zeros = sb("zeros", [P, D], bf16)

        w_raw = [t[:, 0:KD * 2 * H + KH * D] for t in (scan, work)]
        w13_raw = [w[:, 0:KD * 2 * H].rearrange("p (m k n) -> p m k n", m=2, k=KD) for w in w_raw]
        w2_raw = [w[:, KD * 2 * H:].rearrange("p (k n) -> p k n", k=KH) for w in w_raw]

        def split_views(t):
            flat = t[:].rearrange("p a k n -> p (a k n)")
            n = KD * 2 * H + KH * D
            return ([flat[:, s * n:s * n + KD * 2 * H] for s in range(2)],
                    [flat[:, s * n + KD * 2 * H:(s + 1) * n] for s in range(2)])

        w13_hi, w2_hi = split_views(sw_hi)
        w13_lo, w2_lo = split_views(sw_lo)

        psum = ctx.enter_context(nc.psum_tensor("psum", [P, 8, 512], fp32))

        edges_in, x_in, w_in = sem("edges_in"), sem("x_in"), sem("w_in")
        consts, pool_steps = sem("consts"), sem("pool_steps")
        w_hi_done, w_split = sem("w_hi_done"), sem("w_split")
        gate_t = sem("gate_t")
        onehot_ready, totals_ready, scan_done, prefix_ready = (
            sem("onehot_ready"), sem("totals_ready"), sem("scan_done"), sem("prefix_ready"))
        xn_ready, xt_ready, xth_ready, xtl_ready, hw_ready, hw_evac = (
            sem("xn_ready"), sem("xt_ready"), sem("xth_ready"), sem("xtl_ready"), sem("hw_ready"), sem("hw_evac"))
        hw_stored = [sem(f"hw_stored{s}") for s in range(2)]
        sort_plain, sort_dve, sort_act, sort_used, sorted_ready = (
            sem("sort_plain"), sem("sort_dve"), sem("sort_act"), sem("sort_used"), sem("sorted_ready"))
        dve_rank, dve_ln, dve_block, dve_route, dve_tok = (
            sem("dve_rank"), sem("dve_ln"), sem("dve_block"), sem("dve_route"), sem("dve_tok"))
        staged, xstaged = sem("staged"), sem("xstaged")
        gathered = [sem(f"gathered{j}") for j in range(QUADS_RING)]
        ghi_ready, split_ready, agg_used, agg_ready, x1_done = (
            sem("ghi_ready"), sem("split_ready"), sem("agg_used"), sem("agg_ready"), sem("x1_done"))
        xn2_ready, xn2_stored = sem("xn2_ready"), sem("xn2_stored")
        t2_ready, x2h_ready, x2l_ready, h_ready, silu_ready, hs_ready = (
            sem("t2_ready"), sem("x2h_ready"), sem("x2l_ready"), sem("h_ready"), sem("silu_ready"), sem("hs_ready"))
        logits_ready = sem("logits_ready")
        hT_ready, hTh_ready, hTl_ready, y_ready, shared_done = (
            sem("hT_ready"), sem("hTh_ready"), sem("hTl_ready"), sem("y_ready"), sem("shared_done"))
        top_ready, sig_ready, pairs_oh, rtot, rscan, rpre, texp_c, texp_t, tables = (
            sem("top_ready"), sem("sig_ready"), sem("pairs_oh"), sem("rtot"), sem("rscan"), sem("rpre"),
            sem("texp_c"), sem("texp_t"), sem("tables"))
        tsort_ready, tsort_used = sem("tsort_ready"), sem("tsort_used")
        w13_loaded = [sem(f"w13_loaded{s}") for s in range(2)]
        w2_loaded = [sem(f"w2_loaded{s}") for s in range(2)]
        xg_in = [sem(f"xg_in{s}") for s in range(2)]
        w13h, w13l, w2h, w2l = sem("w13h"), sem("w13l"), sem("w2h"), sem("w2l")
        ext_ready, exh_ready, exl_ready, h13_ready, sil_ready, eh_ready = (
            sem("ext_ready"), sem("exh_ready"), sem("exl_ready"), sem("h13_ready"), sem("sil_ready"), sem("eh_ready"))
        eht_ready, ehth_ready, ehtl_ready, ey_ready, ey_evac = (
            sem("eht_ready"), sem("ehth_ready"), sem("ehtl_ready"), sem("ey_ready"), sem("ey_evac"))
        ys_stored = [sem(f"ys_stored{s}") for s in range(2)]
        ys_zeroed = sem("ys_zeroed")
        cstaged, held = sem("cstaged"), sem("held")
        yg_in = [sem(f"yg_in{s}") for s in range(HALF)]
        combined, out_stored, comb_steps = sem("combined"), sem("out_stored"), sem("comb_steps")

        def hold(engine):
            engine.sem_inc(held, 1)

        def mm3(pe, o, a_hi, a_lo, b_hi, b_lo, first, last):
            pe.matmul(o, a_hi, b_hi, start=first, stop=False)
            pe.matmul(o, a_lo, b_hi, start=False, stop=False)
            return pe.matmul(o, a_hi, b_lo, start=False, stop=last)

        def rows4(ap, k, n):
            return ap.rearrange("p (m n) -> p n m", n=n)[:, k, :]

        def within(b, lag):
            return not isinstance(b, int) or lag <= b < TILES + lag

        def blocks(engine, aggregate, boundary):
            for b in range(DRAIN):
                aggregate(b)
                boundary(b)
            with engine.Fori(DRAIN, TILES) as b:
                aggregate(b)
                boundary(b)
            for b in range(TILES, TILES + DRAIN):
                boundary(b)

        block = ctx.enter_context(nc.Block())

        @block.sync
        def _(sp):
            sp.dma_start(src_i, src.rearrange("(p k) -> p k", p=P)).then_inc(edges_in, 16)
            sp.dma_start(dst_i, dst.rearrange("(p k) -> p k", p=P)).then_inc(edges_in, 16)
            sp.dma_start(ew_f, edge_weight.rearrange("(p k) -> p k", p=P)).then_inc(edges_in, 16)
            sp.dma_start(acc[:], x.rearrange("(t p) d -> p t d", p=P)).then_inc(x_in, 16)
            for m, w in enumerate((gnn_w, sw1, sw3, sw2)):
                sp.dma_start(raw[:, m], w.rearrange("(p k) n -> p k n", p=P)).then_inc(w_in, 16)
            sp.dma_start(gate_f, gate_w).then_inc(w_in, 16)
            sp.dma_start(bias_f, gnn_bias.rearrange("(a d) -> a d", a=1)).then_inc(w_in, 16)
            sp.wait_ge(consts, 1)
            zero_row = zeros[:].bitcast(fp32)
            zero_part = 16
            zero_sems = [ys_zeroed] * (2 * MAX_TILES // zero_part - 2) + ys_stored
            for q, zeroed in enumerate(zero_sems):
                sp.dma_start(ys_dram.rearrange("(p r) (h n) -> p (r h) n", p=P, h=2)[:, zero_part * q:zero_part * (q + 1)],
                             zero_row.unsqueeze(1).to_broadcast([P, zero_part, D // 2])).then_inc(zeroed, 16)
            with sp.Fori(0, TILES) as t:
                sp.wait_ge(xn2_ready, t + 1)
                sp.dma_start(xn_dram[bass.ds(t * P, P), :], xn[:, 0]).then_inc(xn2_stored, 16)
            sp.wait_ge(tables, 1)
            middle = sp.value_load(groups[0:1, 0:1], min_val=1, max_val=MAX_TILES // 2 - 2)
            with sp.Fori(0, middle + 2) as g:
                for s in range(2):
                    e = sp.value_load(texp_row[0:1, bass.ds(2 * g + s, 1)], min_val=0, max_val=EXPERTS - 1)
                    sp.wait_ge(w13l, 2 * g + s + 1)
                    for m, w in enumerate((w1, w3)):
                        sp.dma_start(w13_raw[s][:, m], w[bass.ds(e, 1)].rearrange("a (p k) n -> p (a k) n", p=P)
                                     ).then_inc(w13_loaded[s], 16)
                    sp.wait_ge(w2l, 2 * g + s + 1)
                    sp.dma_start(w2_raw[s], w2[bass.ds(e, 1)].rearrange("a (p k) n -> p (a k) n", p=P)
                                 ).then_inc(w2_loaded[s], 16)
            with sp.Fori(0, TILES) as t:
                sp.wait_ge(combined, t + (1 + HALF // TOPK))
                sp.dma_start(out[bass.ds(t * P, P), :], acc[:, bass.ds(t, 1), :]).then_inc(out_stored, 16)
            sp.wait_ge(out_stored, 16 * TILES)

        @block.gpsimd
        def _(pool):
            st = Steps(pool, pool_steps)
            st.add(pool.memset(ident[:], 0.0))
            st.add(pool.memset(before_neg[:], -1.0))
            st.add(pool.iota(iota_i, [[1, CHUNKS]], base=0, channel_multiplier=0))
            st.add(pool.iota(tok_i[:], [[P, TILES]], base=0, channel_multiplier=1))
            st.wait()
            st.add(pool.affine_select(out=ident[:], in_=ident[:], compare_op=ALU.not_equal, fill=1.0,
                                      base=0, pattern=[[-1, P]], channel_multiplier=1))
            st.add(pool.affine_select(out=before_neg[:], in_=before_neg[:], compare_op=ALU.is_ge, fill=0.0,
                                      base=0, pattern=[[-1, P]], channel_multiplier=1))
            st.add(pool.tensor_copy(iota_f[:], iota_i))
            st.add(pool.tensor_copy(tok_f[:], tok_i[:]))
            st.add(pool.memset(ones_b[:], 1.0))
            st.add(pool.memset(zeros[:], 0.0))
            st.wait()
            pool.sem_inc(consts, 1)
            pool.wait_ge(sorted_ready, 1)
            for s in range(2):
                pool.wait_ge(hw_stored[s], 16 * (TILES // 2))
            pool.tensor_copy(stage[:], sdst[:, 0:RING]).then_inc(staged, 1)
            pool.wait_ge(staged, 1)
            for j in range(1, QUADS_RING):
                pool.indirect_dma_start(ring[:, QUAD * j], None, hw_dram, bass.IndirectOffsetOnAxis(stage[:, 0:1], 0)
                                        ).then_inc(gathered[j], 16)
            for j in range(1, QUADS_RING):
                pool.wait_ge(gathered[j], 16)
            n_rounds = pool.value_load(rounds[0:1, 0:1], min_val=1, max_val=CHUNKS // RING)
            with pool.Fori(0, n_rounds) as i:
                for j in range(QUADS_RING):
                    pool.wait_ge(split_ready, RING * i + QUAD * (j + 1))
                    pool.tensor_copy(stage[:, QUAD * j:QUAD * (j + 1)], sdst[:, bass.ds(RING * i + QUAD * j, QUAD)]
                                     ).then_inc(staged, 1)
                    pool.wait_ge(staged, QUADS_RING * i + (j + 2))
                    hold(pool)
                    for r in range(QUAD * j, QUAD * (j + 1)):
                        pool.indirect_dma_start(ring[:, r], None, hw_dram, bass.IndirectOffsetOnAxis(stage[:, r:r + 1], 0)
                                                ).then_inc(gathered[j], 16)
            pool.wait_ge(tables, 1)
            pool.wait_ge(xn2_stored, 16 * TILES)
            middle = pool.value_load(groups[0:1, 0:1], min_val=1, max_val=MAX_TILES // 2 - 2)
            with pool.Fori(0, middle + 2) as g:
                for s in range(2):
                    pool.wait_ge(ext_ready, 2 * g + s + 1)
                    pool.tensor_copy(stage[:, s:s + 1], tok_sorted[:, bass.ds(2 * g + s, 1)]).then_inc(xstaged, 1)
                    pool.wait_ge(xstaged, 2 * g + s + 1)
                    hold(pool)
                    pool.indirect_dma_start(hwb[:, s], None, xn_dram,
                                            bass.IndirectOffsetOnAxis(stage[:, s:s + 1], 0)).then_inc(xg_in[s], 16)
            for s in range(2):
                pool.wait_ge(ys_stored[s], 16 * middle + 48)
            hold(pool)
            with pool.Fori(0, TILES * TOPK // HALF) as i:
                pool.wait_ge(combined, (i + 1) * (HALF // TOPK))
                pool.tensor_copy(stage[:, 0:HALF], comb_idx[:].rearrange("p t k -> p (t k)")[:, bass.ds(i * HALF, HALF)]
                                 ).then_inc(cstaged, 1)
                pool.wait_ge(cstaged, i + 1)
                hold(pool)
                for r in range(HALF):
                    pool.indirect_dma_start(ring[:, r], None, ys_dram,
                                            bass.IndirectOffsetOnAxis(stage[:, r:r + 1], 0)
                                            ).then_inc(yg_in[r], 16)

        @block.tensor
        def _(pe):
            pe.sem_inc(sort_used, 4)
            pe.sem_inc(agg_used, QUAD)
            pe.sem_inc(tsort_used, 2)
            pe.sem_inc(ext_ready, 2)
            pe.sem_inc(h13_ready, 2)
            pe.sem_inc(ey_ready, 2)
            pe.wait_ge(consts, 1)
            pe.wait_ge(onehot_ready, 1)
            for b in range(8):
                pe.matmul(psum[:, b], ones_b[:], onehot[:, 512 * b:512 * b + 512], start=True, stop=True
                          ).then_inc(totals_ready, 1)
            for b in range(8):
                pe.wait_ge(scan_done, b + 1)
                pe.matmul(psum[:, b], before_neg[:], onehot[:, 512 * b:512 * b + 512], start=True, stop=True
                          ).then_inc(prefix_ready, 1)
            pe.wait_ge(w_in, 96)
            pe.wait_ge(scan_done, 9)
            for k in range(KD):
                last = pe.transpose(psum[:, 4, EXPERTS * k:EXPERTS * (k + 1)], rows4(gate_f, k, KD),
                                    ident[0:EXPERTS, 0:EXPERTS])
            last.then_inc(gate_t, 1)
            pe.wait_ge(w_split, 1)
            def product(i):
                for s in range(2):
                    pe.wait_ge(xn_ready, 2 * i + s + 1)
                    for k in range(KD):
                        last = pe.transpose(psum[:, 4 + s, P * k:P * (k + 1)], rows4(xn[:, s], k, KD), ident[:])
                    last.then_inc(xt_ready, 1)
                for s in range(2):
                    pe.wait_ge(xtl_ready, 2 * i + s + 1)
                    if within(i, 1):
                        pe.wait_ge(hw_evac, 2 * i)
                    for k in range(KD):
                        last = mm3(pe, psum[:, 6 + s], xt_hi[:, s, k], xt_lo[:, s, k], gw_hi[:, k], gw_lo[:, k],
                                   k == 0, k == KD - 1)
                    last.then_inc(hw_ready, 1)

            product(0)
            with pe.Fori(1, TILES // 2) as i:
                product(i)
            for f in range(4):
                pe.matmul(psum[:, f, 0:CHUNKS], zeros[:, 0:P], zeros[:, 0:CHUNKS], start=True, stop=True)
            with pe.Fori(0, EC // 4) as i:
                for s in range(2):
                    pe.wait_ge(sort_dve, 2 * i + s + 1)
                    for f in range(4):
                        if f == 2:
                            pe.wait_ge(sort_act, 2 * i + s + 1)
                        for c in range(2):
                            last = pe.matmul(psum[:, f, 0:CHUNKS], lane_oh[:, s, c, f], tile_oh[:, s, c],
                                             start=False, stop=True, skip_group_check=True)
                    last.then_inc(sort_used, 2)
            pe.wait_ge(sorted_ready, 1)

            def boundary(b):
                if within(b, 1):
                    pe.wait_ge(x2l_ready, b)
                    if within(b, 2):
                        pe.wait_ge(hs_ready, b - 1)
                    for k in range(KD):
                        mm3(pe, psum[:, 2, 0:EXPERTS], xt_hi[:, 0, k], xt_lo[:, 0, k], gt_hi[:, k], gt_lo[:, k],
                            k == 0, k == KD - 1)
                    for m in range(2):
                        for k in range(KD):
                            last = mm3(pe, psum[:, 3 + m], xt_hi[:, 0, k], xt_lo[:, 0, k],
                                       sw_hi[:, m, k], sw_lo[:, m, k], k == 0, k == KD - 1)
                    last.then_inc(h_ready, 1)
                if within(b, 3):
                    pe.wait_ge(hTl_ready, b - 2)
                    if within(b, 4):
                        pe.wait_ge(shared_done, b - 3)
                    for k in range(KD):
                        last = mm3(pe, psum[:, 6], sht_hi[:, k], sht_lo[:, k], sw_hi[:, 2, k], sw_lo[:, 2, k],
                                   k == 0, k == KD - 1)
                    last.then_inc(y_ready, 1)
                if within(b, 2):
                    pe.wait_ge(hs_ready, b - 1)
                    for k in range(KD):
                        last = pe.transpose(psum[:, 5, P * k:P * (k + 1)], rows4(hid[:, 1], k, KD), ident[:])
                    last.then_inc(hT_ready, 1)
                if within(b, 0):
                    pe.wait_ge(xn2_ready, b + 1)
                    for k in range(KD):
                        last = pe.transpose(psum[:, 1, P * k:P * (k + 1)], rows4(xn[:, 0], k, KD), ident[:])
                    last.then_inc(t2_ready, 1)

            def aggregate(b):
                first = pe.value_load(quad_tab[0:1, bass.ds(b, 1)], min_val=0, max_val=QUADS)
                end = pe.value_load(quad_tab[0:1, bass.ds(b + 1, 1)], min_val=0, max_val=QUADS)
                if within(b, 1):
                    pe.wait_ge(x1_done, b)
                pe.matmul(psum[:, 0], one_r[:], bias_hi[:], start=True, stop=True)
                with pe.Fori(first, end) as q:
                    for s in range(QUAD):
                        pe.wait_ge(split_ready, QUAD * q + (RING + s + 1))
                        pe.matmul(psum[:, 0], row_oh[:, s], g_hi[:, s], start=False, stop=True, skip_group_check=True)
                        pe.matmul(psum[:, 0], row_oh[:, s], g_lo[:, s], start=False, stop=True, skip_group_check=True
                                  ).then_inc(agg_used, 1)
                pe.matmul(psum[:, 0], one_r[:], bias_lo[:], start=False, stop=True, skip_group_check=True
                          ).then_inc(agg_ready, 1)

            blocks(pe, aggregate, boundary)
            pe.wait_ge(pairs_oh, 1)
            for b in range(2):
                last = pe.matmul(psum[:, b], ones_b[:], onehot[:, 512 * b:512 * b + 512], start=True, stop=True)
            last.then_inc(rtot, 1)
            for b in range(2):
                last = pe.matmul(psum[:, 2 + b], before_neg[:], onehot[:, 512 * b:512 * b + 512], start=True, stop=True)
            last.then_inc(rpre, 1)
            pe.wait_ge(texp_c, 1)
            pe.matmul(psum[0:1, 5, 0:P], texp_f[:, 1:2], ident[:], start=True, stop=True).then_inc(texp_t, 1)
            pe.matmul(psum[:, 4, 0:MAX_TILES], zeros[:, 0:P], zeros[:, 0:MAX_TILES], start=True, stop=True)
            with pe.Fori(0, TILES) as t:
                for k in range(TOPK):
                    pe.wait_ge(tsort_ready, 2 * t + k + 1)
                    pe.matmul(psum[:, 4, 0:MAX_TILES], lane_oh[:, k, 0, 0], tile_oh[:, k, 0, 0:MAX_TILES],
                              start=False, stop=True, skip_group_check=True).then_inc(tsort_used, 1)
            pe.wait_ge(tables, 1)
            middle = pe.value_load(groups[0:1, 0:1], min_val=1, max_val=MAX_TILES // 2 - 2)

            def x_transpose(b, c):
                s = c % 2
                pe.wait_ge(xg_in[s], b * 8 + (c - s) * 8 + 16)
                for k in range(KD):
                    last = pe.transpose(psum[:, s, P * k:P * (k + 1)], rows4(hwb[:, s], k, KD), ident[:])
                last.then_inc(ext_ready, 1)

            def up(b, c):
                s = c % 2
                pe.wait_ge(exl_ready, b + (c + 1))
                pe.wait_ge(w13l, b + (c + 3))
                for k in range(KD):
                    last = mm3(pe, psum[:, 2 + s], xt_hi[:, s, k], xt_lo[:, s, k],
                               w13_hi[s].rearrange("p (m k n) -> p m k n", m=2, k=KD)[:, :, k],
                               w13_lo[s].rearrange("p (m k n) -> p m k n", m=2, k=KD)[:, :, k],
                               k == 0, k == KD - 1)
                last.then_inc(h13_ready, 1)

            def h_transpose(b, c):
                s = c % 2
                pe.wait_ge(eh_ready, b + (c + 1))
                for k in range(KH):
                    last = pe.transpose(psum[:, 4 + s, P * k:P * (k + 1)], rows4(hid[:, s, H:2 * H], k, KH), ident[:])
                last.then_inc(eht_ready, 1)

            def down(b, c):
                s = c % 2
                pe.wait_ge(ehtl_ready, b + (c + 1))
                pe.wait_ge(w2l, b + (c + 3))
                pe.wait_ge(ey_evac, b + (c + 1))
                for k in range(KH):
                    last = mm3(pe, psum[:, 6 + s], ht_hi[:, 2 * s + k, 0:P], ht_lo[:, 2 * s + k, 0:P],
                               w2_hi[s].rearrange("p (k n) -> p k n", k=KH)[:, k],
                               w2_lo[s].rearrange("p (k n) -> p k n", k=KH)[:, k], k == 0, k == KH - 1)
                last.then_inc(ey_ready, 1)

            def step(b, c, x_ahead=True, before=True):
                if x_ahead:
                    x_transpose(b, c + 1)
                up(b, c)
                if before:
                    down(b, c - 1)
                h_transpose(b, c)

            x_transpose(0, 0)
            step(0, 0, before=False)
            with pe.Fori(0, middle) as g:
                step(2 * g, 1)
                step(2 * g, 2)
            rest = 2 * middle
            step(rest, 1)
            step(rest, 2)
            step(rest, 3, x_ahead=False)
            down(rest, 3)

        @block.scalar
        def _(act):
            act.sem_inc(ey_evac, 2)
            act.wait_ge(w_in, 96)
            act.wait_ge(consts, 1)
            nc.scalar.copy(gw_hi[:], raw[:, 0]).then_inc(w_hi_done, 1)
            for m in range(3):
                nc.scalar.copy(sw_hi[:, m], raw[:, m + 1]).then_inc(w_hi_done, 1)
            nc.scalar.copy(bias_hi[:], bias_f).then_inc(w_hi_done, 1)
            nc.scalar.copy(one_r[:], ones_b[0:1, :]).then_inc(w_hi_done, 1)
            act.wait_ge(gate_t, 1)
            nc.scalar.copy(gt_hi[:], psum[:, 4, 0:KD * EXPERTS].rearrange("p (k e) -> p k e", k=KD)
                           ).then_inc(w_hi_done, 1)

            def product(i):
                for s in range(2):
                    act.wait_ge(xt_ready, 2 * i + s + 1)
                    nc.scalar.copy(xt_hi[:, s], psum[:, 4 + s].rearrange("p (k n) -> p k n", k=KD)
                                   ).then_inc(xth_ready, 1)
                for s in range(2):
                    act.wait_ge(hw_ready, 2 * i + s + 1)
                    if within(i, 1):
                        act.wait_ge(hw_stored[s], 16 * i)
                    nc.scalar.copy(hwb[:, s], psum[:, 6 + s]).then_inc(hw_evac, 1)
                    act.wait_ge(hw_evac, 2 * i + s + 1)
                    act.dma_start(hw_dram[bass.ds((2 * i + s) * P, P), :], hwb[:, s]).then_inc(hw_stored[s], 16)

            product(0)
            with act.Fori(1, TILES // 2) as i:
                product(i)
            with act.Fori(0, EC // 4) as i:
                for s in range(2):
                    act.wait_ge(sort_plain, 2 * i + s + 1)
                    for c in range(2):
                        for f in (2, 3):
                            last = nc.scalar.activation(lane_oh[:, s, c, f], lane_plain[:, s, c], ACT.Copy,
                                                        scale=rec[:, f, bass.ds(4 * i + 2 * s + c, 1)])
                    last.then_inc(sort_act, 1)
            act.wait_ge(sorted_ready, 1)

            def aggregate(b):
                first = act.value_load(quad_tab[0:1, bass.ds(b, 1)], min_val=0, max_val=QUADS)
                end = act.value_load(quad_tab[0:1, bass.ds(b + 1, 1)], min_val=0, max_val=QUADS)
                with act.Fori(first, end) as q:
                    act.wait_ge(gathered[0], (q // QUADS_RING) * (16 * QUAD) + 16 * QUAD)
                    for j in range(1, QUADS_RING):
                        act.wait_ge(gathered[j], ((q + (QUADS_RING - j)) // QUADS_RING) * (16 * QUAD) + 16)
                    for s in range(QUAD):
                        act.wait_ge(agg_used, QUAD * q + (s + 1))
                        nc.scalar.activation(g_hi[:, s], ring[:, bass.ds((q % QUADS_RING) * QUAD + s, 1), :], ACT.Copy,
                                             scale=sew[:, bass.ds(QUAD * q + s, 1)]).then_inc(ghi_ready, 1)

            def boundary(b):
                if within(b, 1):
                    act.wait_ge(t2_ready, b)
                    if within(b, 2):
                        act.wait_ge(h_ready, b - 1)
                    nc.scalar.copy(xt_hi[:, 0], psum[:, 1].rearrange("p (k n) -> p k n", k=KD)).then_inc(x2h_ready, 1)
                if within(b, 2):
                    act.wait_ge(h_ready, b - 1)
                    if within(b, 3):
                        act.wait_ge(hs_ready, b - 2)
                    nc.scalar.activation(hid[:, 0], psum[:, 3], ACT.Silu).then_inc(silu_ready, 1)
                    nc.scalar.copy(logits[:, bass.ds(b - 2, 1), :], psum[:, 2, 0:EXPERTS]).then_inc(logits_ready, 1)
                if within(b, 3):
                    act.wait_ge(hT_ready, b - 2)
                    if within(b, 4):
                        act.wait_ge(y_ready, b - 3)
                    nc.scalar.copy(sht_hi, psum[:, 5].rearrange("p (k n) -> p k n", k=KD)).then_inc(hTh_ready, 1)

            blocks(act, aggregate, boundary)
            act.wait_ge(top_ready, 1)
            nc.scalar.activation(r_small[:, 0], top8[:, :, 0:TOPK].rearrange("p t k -> p k t"), ACT.Sigmoid
                                 ).then_inc(sig_ready, 1)
            act.wait_ge(tables, 1)
            middle = act.value_load(groups[0:1, 0:1], min_val=1, max_val=MAX_TILES // 2 - 2)

            def split13(b, c):
                s = c % 2
                act.wait_ge(w13_loaded[s], b * 16 + (c - s) * 16 + 32)
                act.wait_ge(h13_ready, b + (c + 1))
                nc.scalar.copy(w13_hi[s], w_raw[s][:, 0:KD * 2 * H]).then_inc(w13h, 1)

            def split2(b, c):
                s = c % 2
                act.wait_ge(w2_loaded[s], b * 8 + (c - s) * 8 + 16)
                act.wait_ge(ey_ready, b + (c + 1))
                nc.scalar.copy(w2_hi[s], w_raw[s][:, KD * 2 * H:]).then_inc(w2h, 1)

            def x_high(b, c):
                s = c % 2
                act.wait_ge(ext_ready, b + (c + 3))
                nc.scalar.copy(xt_hi[:, s], psum[:, s].rearrange("p (k n) -> p k n", k=KD)).then_inc(exh_ready, 1)

            def h_high(b, c):
                s = c % 2
                act.wait_ge(eht_ready, b + (c + 1))
                nc.scalar.copy(ht_hi[:, 2 * s:2 * s + 2, 0:P], psum[:, 4 + s, 0:H].rearrange("p (k n) -> p k n", k=KH)
                               ).then_inc(ehth_ready, 1)

            def silu(b, c):
                s = c % 2
                act.wait_ge(h13_ready, b + (c + 3))
                nc.scalar.activation(hid[:, s, 0:H], psum[:, 2 + s, 0:H], ACT.Silu).then_inc(sil_ready, 1)

            def store(b, c):
                s = c % 2
                act.wait_ge(ey_ready, b + (c + 3))
                act.wait_ge(ys_stored[s], b * 8 + (c - s) * 8 + 16)
                nc.scalar.copy(xn[:, s], psum[:, 6 + s]).then_inc(ey_evac, 1)
                act.wait_ge(ey_evac, b + (c + 3))
                act.dma_start(ys_dram[bass.ds(b * P + c * P, P), :], xn[:, s]).then_inc(ys_stored[s], 16)

            def step(b, c, before=True, ahead=2):
                if ahead >= 1:
                    x_high(b, c + 1)
                silu(b, c)
                if ahead == 2:
                    split13(b, c + 2)
                h_high(b, c)
                if before:
                    store(b, c - 1)
                if ahead >= 1:
                    split2(b, c + 1)

            act.wait_ge(ys_zeroed, 16 * (2 * MAX_TILES // 16 - 2))
            for s in range(2):
                act.wait_ge(ys_stored[s], 16)
            split13(0, 0)
            x_high(0, 0)
            split13(0, 1)
            split2(0, 0)
            step(0, 0, before=False)
            with act.Fori(0, middle) as g:
                step(2 * g, 1)
                step(2 * g, 2)
            rest = 2 * middle
            step(rest, 1)
            step(rest, 2, ahead=1)
            step(rest, 3, ahead=0)
            store(rest, 3)

        @block.vector
        def _(v):
            v.sem_inc(split_ready, RING)
            v.sem_inc(w13l, 2)
            v.sem_inc(w2l, 2)
            v.sem_inc(combined, HALF // TOPK)

            def rsqrt(step, o, a, b, width):
                step(v.tensor_scalar(a[0], a[0], EPS, None, ALU.add))
                step.add(v.tensor_scalar(a[1], a[0], 0.25, None, ALU.mult))
                step.add(v.tensor_scalar(a[2], a[0], 0.0625, None, ALU.mult))
                step(v.tensor_scalar(b.bitcast(i32), a[0].bitcast(i32), 1, None, ALU.logical_shift_right))
                step(v.tensor_scalar(o.bitcast(i32), b.bitcast(i32), -1.0, float(RSQRT_GUESS), ALU.mult, ALU.add))
                for k in range(3):
                    if width == 1:
                        step(v.scalar_tensor_tensor(b, o, a[k], o, ALU.mult, ALU.mult))
                    else:
                        step(v.tensor_tensor(b, a[k], o, ALU.mult))
                        step(v.tensor_tensor(b, b, o, ALU.mult))
                    step(v.scalar_tensor_tensor(o, b, -3.0, o, ALU.add, ALU.mult))
                step(v.tensor_scalar(o, o, -0.125, None, ALU.mult))

            st = Steps(v, dve_rank)
            v.wait_ge(edges_in, 48)
            st.add(v.tensor_scalar(block_i, src_i, BLOCK_SHIFT, None, ALU.logical_shift_right))
            st.add(v.tensor_scalar(lane_i, src_i, P - 1, None, ALU.bitwise_and))
            st.add(v.tensor_copy(ew_r, ew_f))
            st.add(v.tensor_copy(rec[:, 0], dst_i))
            st.wait()
            st.add(v.tensor_copy(block_f, block_i))
            st.add(v.tensor_copy(rec[:, 1], lane_i))
            st.add(v.tensor_copy(rec[:, 2], ew_r.bitcast(fp32)))
            st.add(v.tensor_tensor(rec[:, 3], ew_f, ew_r.bitcast(fp32), ALU.subtract))
            st.wait()
            oh3 = onehot[:].rearrange("p (b k) -> p b k", b=TILES)
            for b in range(TILES):
                last = v.tensor_scalar(oh3[:, b], block_f, float(b), None, ALU.is_equal)
            last.then_inc(onehot_ready, 1)
            v.wait_ge(consts, 1)
            for b in range(8):
                v.wait_ge(totals_ready, b + 1)
                v.tensor_tensor_scan(scan[:, 512 * b:512 * b + 512], psum[:, b], zeros[:],
                                     0.0 if b == 0 else scan[:, 512 * b - 1:512 * b], ALU.add, ALU.add
                                     ).then_inc(scan_done, 1)
                v.wait_ge(scan_done, b + 1)
            scan3 = scan[:].rearrange("p (b k) -> p b k", b=TILES)
            last_count = scan3[:, :, EC - 1]
            cnt, n_quads, p_end, p_start, corr, tmp = (ends[:, j] for j in range(6))
            st.add(v.tensor_copy(cnt[:, 0:1], last_count[:, 0:1]))
            st.add(v.tensor_tensor(cnt[:, 1:], last_count[:, 1:], last_count[:, 0:TILES - 1], ALU.subtract))
            st.wait()
            st(v.tensor_scalar(tmp, cnt, float(QUAD * P - 1), None, ALU.add))
            st(v.tensor_copy(ends_i[:], tmp))
            st(v.tensor_scalar(ends_i[:], ends_i[:], QUAD_SHIFT, None, ALU.logical_shift_right))
            st(v.tensor_copy(n_quads, ends_i[:]))
            st(v.tensor_scalar(n_quads, n_quads, 1.0, None, ALU.max))
            st(v.tensor_tensor_scan(p_end, n_quads, zeros[:, 0:TILES], 0.0, ALU.add, ALU.add))
            st(v.tensor_tensor(p_start, p_end, n_quads, ALU.subtract))
            st.add(v.tensor_copy(quad_tab[:, 0:TILES], p_start))
            st(v.tensor_scalar(tmp[:, 0:1], p_end[:, TILES - 1:TILES], float(QUADS_RING - 1), None, ALU.add))
            st(v.tensor_copy(ends_i[:, 0:1], tmp[:, 0:1]))
            st(v.tensor_scalar(rounds[:], ends_i[:, 0:1], ROUND_SHIFT, None, ALU.logical_shift_right))
            st(v.tensor_scalar(quad_tab[:, TILES:], rounds[:], float(QUADS_RING), None, ALU.mult))
            st(v.tensor_tensor(corr, last_count, cnt, ALU.subtract))
            st(v.scalar_tensor_tensor(corr, p_start, float(QUAD * P), corr, ALU.mult, ALU.subtract))
            work3 = work[:].rearrange("p (b k) -> p b k", b=TILES)
            for b in range(TILES):
                v.wait_ge(prefix_ready, b // 2 + 1)
                st.add(v.scalar_tensor_tensor(work3[:, b], scan3[:, b], corr[:, b:b + 1],
                                              psum[:, b // 2, EC * (b % 2):EC * (b % 2 + 1)], ALU.add, ALU.add))
            st.wait()
            v.sem_inc(scan_done, 1)
            st(v.tensor_tensor(work[:], work[:], onehot[:], ALU.mult))
            st(v.tensor_reduce(pos_f, work3.rearrange("p b k -> p k b"), AX.X, ALU.add))
            st(v.tensor_copy(pos_i, pos_f))
            st.add(v.tensor_scalar(block_i, pos_i, BLOCK_SHIFT, None, ALU.logical_shift_right))
            st.add(v.tensor_scalar(lane_i, pos_i, P - 1, None, ALU.bitwise_and))
            st.wait()
            st.add(v.tensor_copy(slot_tile[:], block_i))
            st.add(v.tensor_copy(slot_lane[:], lane_i))
            st.wait()
            v.wait_ge(w_in, 96)
            v.wait_ge(w_hi_done, 4)
            v.tensor_tensor(gw_lo[:], raw[:, 0], gw_hi[:].bitcast(fp32), ALU.subtract)
            for m in range(3):
                v.tensor_tensor(sw_lo[:, m], raw[:, m + 1], sw_hi[:, m].bitcast(fp32), ALU.subtract)
            v.wait_ge(w_hi_done, 7)
            v.tensor_tensor(bias_lo[:], bias_f, bias_hi[:].bitcast(fp32), ALU.subtract)
            v.tensor_tensor(gt_lo[:], psum[:, 4, 0:KD * EXPERTS].rearrange("p (k e) -> p k e", k=KD),
                            gt_hi[:].bitcast(fp32), ALU.subtract).then_inc(w_split, 1)
            v.wait_ge(x_in, 16)
            sl = Steps(v, dve_ln)
            for t in range(TILES):
                sl.add(v.bn_stats(stats[:, t], acc[:, t]))
            sl.wait()
            for t in range(TILES):
                sl.add(v.bn_aggr(mv[:, t], stats[:, t]))
            sl.wait()
            sl(v.tensor_copy(newton[:, 0], mv[:, :, 1]))
            rsqrt(sl, rstd[:], [newton[:, k] for k in range(3)], newton[:, 3], TILES)

            def product(i):
                for s in range(2):
                    n = 2 * i + s
                    if within(i, 1):
                        v.wait_ge(xt_ready, 2 * i)
                    v.tensor_scalar(xn[:, s], acc[:, bass.ds(n, 1), :], mv[:, bass.ds(n, 1), 0:1].rearrange("p a b -> p (a b)"),
                                    rstd[:, bass.ds(n, 1)], ALU.subtract, ALU.mult).then_inc(xn_ready, 1)
                for s in range(2):
                    v.wait_ge(xth_ready, 2 * i + s + 1)
                    v.tensor_tensor(xt_lo[:, s], psum[:, 4 + s].rearrange("p (k n) -> p k n", k=KD),
                                    xt_hi[:, s].bitcast(fp32), ALU.subtract).then_inc(xtl_ready, 1)

            product(0)
            with v.Fori(1, TILES // 2) as i:
                product(i)
            v.wait_ge(hw_ready, TILES)
            iota2 = iota_f[:, 0:P].unsqueeze(1).to_broadcast([P, 2, P])
            with v.Fori(0, EC // 4) as i:
                for s in range(2):
                    first = 4 * i + 2 * s
                    v.wait_ge(sort_used, 4 * i + (2 * s + 2))
                    v.tensor_tensor(lane_plain[:, s], iota2,
                                    slot_lane[:, bass.ds(first, 2)].unsqueeze(2).to_broadcast([P, 2, P]),
                                    ALU.is_equal).then_inc(sort_plain, 1)
                    for c in range(2):
                        v.tensor_scalar(tile_oh[:, s, c], iota_f[:], slot_tile[:, bass.ds(first + c, 1)], None,
                                        ALU.is_equal)
                    v.wait_ge(sort_plain, 2 * i + s + 1)
                    v.tensor_tensor(lane_oh[:, s, :, 0:2], lane_plain[:, s].unsqueeze(2).to_broadcast([P, 2, 2, P]),
                                    rec[:, 0:2, bass.ds(first, 2)].rearrange("p f c -> p c f").unsqueeze(3
                                        ).to_broadcast([P, 2, 2, P]), ALU.mult).then_inc(sort_dve, 1)
            v.wait_ge(sort_used, EC + 4)
            sl.add(v.tensor_copy(sdst, psum[:, 0, 0:CHUNKS]))
            sl.add(v.tensor_copy(slane, psum[:, 1, 0:CHUNKS]))
            sl(v.tensor_copy(sew, psum[:, 2, 0:CHUNKS]))
            sl(v.tensor_tensor(sew, sew, psum[:, 3, 0:CHUNKS], ALU.add))
            v.sem_inc(sorted_ready, 1)
            sk = Steps(v, dve_block)

            def row(b):
                return acc[:, bass.ds(b, 1), :].rearrange("p a n -> p (a n)")

            def aggregate(b):
                first = v.value_load(quad_tab[0:1, bass.ds(b, 1)], min_val=0, max_val=QUADS)
                end = v.value_load(quad_tab[0:1, bass.ds(b + 1, 1)], min_val=0, max_val=QUADS)
                with v.Fori(first, end) as q:
                    for s in range(QUAD):
                        v.wait_ge(agg_used, QUAD * q + (s + 1))
                        v.tensor_scalar(row_oh[:, s], iota_f[:, 0:P], slane[:, bass.ds(QUAD * q + s, 1)], None,
                                        ALU.is_equal)
                        v.wait_ge(ghi_ready, QUAD * q + (s + 1))
                        v.scalar_tensor_tensor(g_lo[:, s],
                                               ring[:, bass.ds((q % QUADS_RING) * QUAD + s, 1), :].rearrange("p a n -> p (a n)"),
                                               sew[:, bass.ds(QUAD * q + s, 1)], g_hi[:, s].bitcast(fp32),
                                               ALU.mult, ALU.subtract).then_inc(split_ready, 1)

            def boundary(b):
                if within(b, 1):
                    v.wait_ge(x2h_ready, b)
                    v.tensor_tensor(xt_lo[:, 0], psum[:, 1].rearrange("p (k n) -> p k n", k=KD),
                                    xt_hi[:, 0].bitcast(fp32), ALU.subtract).then_inc(x2l_ready, 1)
                if within(b, 2):
                    v.wait_ge(silu_ready, b - 1)
                    if within(b, 3):
                        v.wait_ge(hT_ready, b - 2)
                    v.wait_ge(logits_ready, b - 1)
                    v.tensor_tensor(hid[:, 1], hid[:, 0], psum[:, 4], ALU.mult).then_inc(hs_ready, 1)
                if within(b, 3):
                    v.wait_ge(hTh_ready, b - 2)
                    v.tensor_tensor(sht_lo, psum[:, 5].rearrange("p (k n) -> p k n", k=KD),
                                    sht_hi.bitcast(fp32), ALU.subtract).then_inc(hTl_ready, 1)
                if within(b, 4):
                    v.wait_ge(y_ready, b - 3)
                    v.tensor_tensor(row(b - 4), row(b - 4), psum[:, 6], ALU.add).then_inc(shared_done, 1)
                if within(b, 0):
                    v.wait_ge(agg_ready, b + 1)
                    v.scalar_tensor_tensor(row(b), psum[:, 0], 0.0, row(b), ALU.max, ALU.add).then_inc(x1_done, 1)
                    sk.base, sk.n = b * NORM_STEPS, 0
                    v.wait_ge(x1_done, b + 1)
                    hold(v)
                    sk.add(v.bn_stats(stats[:, 0], row(b)))
                    sk.wait()
                    hold(v)
                    sk(v.bn_aggr(mv[:, 0], stats[:, 0]))
                    rsqrt(sk, rstd[:, 0:1], [mv[:, 0, 1:2], newton[:, 1, 0:1], newton[:, 2, 0:1]], newton[:, 3, 0:1], 1)
                    assert sk.n == NORM_STEPS, sk.n
                    if within(b, 1):
                        v.wait_ge(xn2_stored, 16 * b)
                        v.wait_ge(t2_ready, b)
                    v.tensor_scalar(xn[:, 0], row(b), mv[:, 0, 0:1], rstd[:, 0:1], ALU.subtract, ALU.mult
                                    ).then_inc(xn2_ready, 1)

            blocks(v, aggregate, boundary)
            v.wait_ge(shared_done, TILES)
            sr = Steps(v, dve_route)
            for t in range(TILES):
                sr.add(v.max(top8[:, t], logits[:, t]))
            sr.wait()
            v.sem_inc(top_ready, 1)
            for t in range(TILES):
                sr.add(v.max_index(idx8[:, t], top8[:, t], logits[:, t]))
            sr.wait()
            score, exp_f, rank, first_tile, valid, slot_c, slot_s, lane_f, tile_f, gate = (
                r_small[:, j] for j in range(10))
            oh_k = [work[:, 1024 * k:1024 * (k + 1)].rearrange("p (e t) -> p e t", t=TILES) for k in range(TOPK)]
            prod = work[:, 2048:3072].rearrange("p (e t) -> p e t", t=TILES)
            ranks = work[:, 3072:4096].rearrange("p (e t) -> p e t", t=TILES)
            oh_sum = onehot[:, 0:EXPERTS * TILES].rearrange("p (e t) -> p e t", t=TILES)
            big = [P, EXPERTS, TILES]
            sr(v.tensor_copy(exp_f, idx8[:, :, 0:TOPK].rearrange("p t k -> p k t")))
            for k in range(TOPK):
                sr.add(v.tensor_tensor(oh_k[k], exp_f[:, k].unsqueeze(1).to_broadcast(big),
                                       iota_f[:, 0:EXPERTS].unsqueeze(2).to_broadcast(big), ALU.is_equal))
            sr.wait()
            v.tensor_tensor(oh_sum, oh_k[0], oh_k[1], ALU.add).then_inc(pairs_oh, 1)
            v.wait_ge(sig_ready, 1)
            sr(v.tensor_tensor(gate[:, 0], score[:, 0], score[:, 1], ALU.add))
            sr(v.tensor_scalar(gate[:, 0], gate[:, 0], 1e-20, None, ALU.add))
            sr(v.reciprocal(gate[:, 1], gate[:, 0]))
            sr(v.tensor_tensor(gate[:, 0], score[:, 0], gate[:, 1], ALU.mult))
            sr(v.tensor_tensor(gate[:, 1], score[:, 1], gate[:, 1], ALU.mult))
            sr(v.tensor_scalar(gate, gate, ROUTE_SCALE, None, ALU.mult))
            v.wait_ge(rtot, 1)
            for b in range(2):
                sr(v.tensor_tensor_scan(scan[:, 512 * b:512 * b + 512], psum[:, b], zeros[:],
                                        0.0 if b == 0 else scan[:, 511:512], ALU.add, ALU.add))
            rscan3 = scan[:, 0:1024].rearrange("p (e t) -> p e t", t=TILES)
            e_end = rscan3[:, :, TILES - 1]
            e_cnt, e_start, e_tiles, t_end, t_start, e_tmp = (x_small[:, j] for j in range(6))
            sr.add(v.tensor_copy(e_cnt[:, 0:1], e_end[:, 0:1]))
            sr(v.tensor_tensor(e_cnt[:, 1:], e_end[:, 1:], e_end[:, 0:EXPERTS - 1], ALU.subtract))
            sr.add(v.tensor_tensor(e_start, e_end, e_cnt, ALU.subtract))
            sr(v.tensor_scalar(e_tmp, e_cnt, float(CAP), float(P - 1), ALU.min, ALU.add))
            sr(v.tensor_copy(x_int, e_tmp))
            sr(v.tensor_scalar(x_int, x_int, BLOCK_SHIFT, None, ALU.logical_shift_right))
            sr(v.tensor_copy(e_tiles, x_int))
            sr(v.tensor_tensor_scan(t_end, e_tiles, zeros[:, 0:EXPERTS], 0.0, ALU.add, ALU.add))
            sr.add(v.tensor_tensor(t_start, t_end, e_tiles, ALU.subtract))
            sr(v.tensor_scalar(x_small[:, 6], t_end, tok_f[:, 0:1], None, ALU.is_le))
            sr(v.tensor_reduce(texp_f[:, 0:1], x_small[:, 6], AX.X, ALU.add))
            v.tensor_scalar(texp_f[:, 1:2], texp_f[:, 0:1], float(EXPERTS - 1), None, ALU.min).then_inc(texp_c, 1)
            sr(v.tensor_scalar(x_small[:, 7, 0:1], t_end[:, EXPERTS - 1:EXPERTS], 1.0, None, ALU.add))
            sr(v.tensor_copy(x_int[:, 0:1], x_small[:, 7, 0:1]))
            sr(v.tensor_scalar(x_int[:, 0:1], x_int[:, 0:1], 1, None, ALU.logical_shift_right))
            sr(v.tensor_copy(x_small[:, 7, 0:1], x_int[:, 0:1]))
            sr(v.tensor_scalar(groups[:], x_small[:, 7, 0:1], -2.0, 1.0, ALU.add, ALU.max))
            v.wait_ge(rpre, 1)
            sr(v.tensor_tensor(ranks, rscan3, psum[:, 2:4].rearrange("p b (e t) -> p (b e) t", t=TILES), ALU.add))
            sr(v.tensor_tensor(ranks, ranks, e_start.unsqueeze(2).to_broadcast(big), ALU.subtract))
            for k in range(TOPK):
                sr(v.tensor_tensor(prod, oh_k[k], ranks, ALU.mult))
                sr(v.tensor_reduce(rank[:, k], prod.rearrange("p e t -> p t e"), AX.X, ALU.add))
                sr(v.tensor_tensor(prod, oh_k[k], t_start.unsqueeze(2).to_broadcast(big), ALU.mult))
                sr(v.tensor_reduce(first_tile[:, k], prod.rearrange("p e t -> p t e"), AX.X, ALU.add))
            sr(v.tensor_scalar(valid, rank, float(CAP), None, ALU.is_lt))
            sr(v.scalar_tensor_tensor(slot_c, first_tile, float(P), rank, ALU.mult, ALU.add))
            sr(v.tensor_tensor(slot_c, slot_c, valid, ALU.mult))
            sr.add(v.tensor_tensor(gate, gate, valid, ALU.mult))
            sr.add(v.tensor_copy(comb_idx[:].rearrange("p t k -> p k t"), slot_c))
            sr(v.tensor_scalar(slot_s, valid, float(-NOWHERE * P), float(NOWHERE * P), ALU.mult, ALU.add))
            sr(v.tensor_tensor(slot_s, slot_s, slot_c, ALU.add))
            sr(v.tensor_copy(r_int[:, 0], slot_s))
            sr.add(v.tensor_scalar(r_int[:, 1], r_int[:, 0], P - 1, None, ALU.bitwise_and))
            sr(v.tensor_scalar(r_int[:, 2], r_int[:, 0], BLOCK_SHIFT, None, ALU.logical_shift_right))
            sr.add(v.tensor_copy(lane_f, r_int[:, 1]))
            sr(v.tensor_copy(tile_f, r_int[:, 2]))
            v.wait_ge(texp_t, 1)
            sr(v.tensor_copy(texp_row, psum[0:1, 5, 0:P]))
            with v.Fori(0, TILES) as t:
                for k in range(TOPK):
                    v.wait_ge(tsort_used, 2 * t + k + 1)
                    v.tensor_scalar(lane_oh[:, k, 0, 0], iota_f[:, 0:P], lane_f[:, k, bass.ds(t, 1)],
                                    tok_f[:, bass.ds(t, 1)], ALU.is_equal, ALU.mult)
                    v.tensor_scalar(tile_oh[:, k, 0, 0:MAX_TILES], iota_f[:, 0:MAX_TILES], tile_f[:, k, bass.ds(t, 1)],
                                    None, ALU.is_equal).then_inc(tsort_ready, 1)
            v.wait_ge(tsort_used, TILES * TOPK + 2)
            sr(v.tensor_copy(tok_sorted, psum[:, 4, 0:MAX_TILES]))
            v.sem_inc(tables, 1)
            middle = v.value_load(groups[0:1, 0:1], min_val=1, max_val=MAX_TILES // 2 - 2)

            def split13(b, c):
                s = c % 2
                v.wait_ge(w13h, b + (c + 1))
                v.tensor_tensor(w13_lo[s], w_raw[s][:, 0:KD * 2 * H], w13_hi[s].bitcast(fp32), ALU.subtract
                                ).then_inc(w13l, 1)

            def split2(b, c):
                s = c % 2
                v.wait_ge(w2h, b + (c + 1))
                v.tensor_tensor(w2_lo[s], w_raw[s][:, KD * 2 * H:], w2_hi[s].bitcast(fp32), ALU.subtract
                                ).then_inc(w2l, 1)

            def x_low(b, c):
                s = c % 2
                v.wait_ge(exh_ready, b + (c + 1))
                v.tensor_tensor(xt_lo[:, s], psum[:, s].rearrange("p (k n) -> p k n", k=KD),
                                xt_hi[:, s].bitcast(fp32), ALU.subtract).then_inc(exl_ready, 1)

            def h_low(b, c):
                s = c % 2
                v.wait_ge(ehth_ready, b + (c + 1))
                v.tensor_tensor(ht_lo[:, 2 * s:2 * s + 2, 0:P], psum[:, 4 + s, 0:H].rearrange("p (k n) -> p k n", k=KH),
                                ht_hi[:, 2 * s:2 * s + 2, 0:P].bitcast(fp32), ALU.subtract).then_inc(ehtl_ready, 1)

            def gated(b, c):
                s = c % 2
                v.wait_ge(sil_ready, b + (c + 1))
                v.tensor_tensor(hid[:, s, H:2 * H], hid[:, s, 0:H], psum[:, 2 + s, H:2 * H], ALU.mult
                                ).then_inc(eh_ready, 1)

            def step(b, c, ahead=2):
                if ahead >= 1:
                    x_low(b, c + 1)
                split2(b, c)
                gated(b, c)
                if ahead == 2:
                    split13(b, c + 2)
                h_low(b, c)

            split13(0, 0)
            x_low(0, 0)
            split13(0, 1)
            step(0, 0)
            with v.Fori(0, middle) as g:
                step(2 * g, 1)
                step(2 * g, 2)
            rest = 2 * middle
            step(rest, 1)
            step(rest, 2, ahead=1)
            step(rest, 3, ahead=0)
            per = HALF // TOPK
            with v.Fori(0, TILES // per) as i:
                for j in range(per):
                    t = per * i + j
                    acc_t = acc[:, bass.ds(t, 1), :].rearrange("p a n -> p (a n)")
                    v.wait_ge(yg_in[2 * j], 16 * i + 16)
                    v.scalar_tensor_tensor(acc_t, ring[:, 2 * j], gate[:, 0, bass.ds(t, 1)], acc_t, ALU.mult, ALU.add
                                           ).then_inc(comb_steps, 1)
                    v.wait_ge(comb_steps, per * i + j + 1)
                    v.wait_ge(yg_in[2 * j + 1], 16 * i + 16)
                    v.scalar_tensor_tensor(acc_t, ring[:, 2 * j + 1], gate[:, 1, bass.ds(t, 1)], acc_t,
                                           ALU.mult, ALU.add).then_inc(combined, 1)


_INS = ['x', 'src', 'dst', 'edge_weight', 'L0_gnn_W', 'L0_gnn_bias', 'L0_ffn_gate_w', 'L0_ffn_w1', 'L0_ffn_w3',
        'L0_ffn_w2', 'L0_ffn_sw1', 'L0_ffn_sw3', 'L0_ffn_sw2']
_OUTS = [((N, D), 'float32')]


def kernel(**inputs):
    import numpy as _np
    import concourse.bacc as _bacc
    from concourse.bass_utils import run_bass_kernel_spmd as _run

    nc = _bacc.Bacc("TRN2", target_bir_lowering=False, num_devices=1)
    arrays, args = {}, []
    for name in _INS:
        a = _np.ascontiguousarray(inputs[name])
        arrays[f"in_{name}_dram"] = a
        args.append(nc.dram_tensor(f"in_{name}_dram", a.shape, mybir.dt.from_np(a.dtype), kind="ExternalInput").ap())
    for i, (shape, dtype) in enumerate(_OUTS):
        dt = mybir.dt.from_np(_np.dtype(dtype))
        args.append(nc.dram_tensor(f"out_{i}_dram", shape, dt, kind="ExternalOutput").ap())
    build_program(nc, *args)
    r = _run(nc, [arrays], core_ids=[0])
    got = tuple(r.results[0][f"out_{i}_dram"] for i in range(len(_OUTS)))
    return got[0]
```

```python
import concourse.bass as bass
from concourse import mybir
from contextlib import ExitStack

fp32 = mybir.dt.float32
f32r = mybir.dt.float32r
bf16 = mybir.dt.bfloat16
i32 = mybir.dt.int32
u32 = mybir.dt.uint32
ALU = mybir.AluOpType
ACT = mybir.ActivationFunctionType
AX = mybir.AxisListType

P = 128
N, D = 2048, 512
E = 32768
EXPERTS, TOPK, H = 64, 2, 256
CAP = 1024
ROUTE_SCALE = 2.5
EPS = 1e-5
TILES = N // P
KD = D // P
KH = H // P
EC = E // P
QUAD = 4
QUADS = E // (QUAD * P) + TILES
CHUNKS = QUAD * QUADS
RING = 16
HALF = RING // 2
QUADS_RING = RING // QUAD
NORM_STEPS = 14
DRAIN = 4
SCATTERED = 144
SORT_COLS = EC - SCATTERED
SCATTER = 8
DVE_FIELDS = 2
BLOCK_SHIFT = 7
QUAD_SHIFT = 9
ROUND_SHIFT = 2
RSQRT_GUESS = 0x5f3759df
MAX_TILES = EXPERTS + N * TOPK // P
RANK_SHIFT = 13
RANKS = 1 << RANK_SHIFT
NOWHERE = 127
YROWS = MAX_TILES * P


class Steps:

    def __init__(self, engine, sem):
        self.engine, self.sem, self.base, self.n = engine, sem, 0, 0

    def add(self, instruction):
        instruction.then_inc(self.sem, 1)
        self.n += 1

    def wait(self):
        self.engine.wait_ge(self.sem, self.base + self.n)

    def __call__(self, instruction):
        self.add(instruction)
        self.wait()


def build_program(nc, x, src, dst, edge_weight, gnn_w, gnn_bias, gate_w, w1, w3, w2, sw1, sw3, sw2, out):
    ctx = ExitStack()
    with ctx:
        def sb(name, shape, dt):
            return ctx.enter_context(nc.sbuf_tensor(name, shape, dt))

        def sem(name):
            return ctx.enter_context(nc.semaphore(name))

        hw_dram = nc.dram_tensor("hw_dram", [N, D], fp32).ap()
        xn_dram = nc.dram_tensor("xn_dram", [N, D], fp32).ap()
        sort_dram = nc.dram_tensor("sort_dram", [P * CHUNKS, 4], fp32).ap()
        ys_dram = nc.dram_tensor("ys_dram", [YROWS, D], fp32).ap()

        acc = sb("acc", [P, TILES, D], fp32)
        raw = sb("raw", [P, 4, KD, D], fp32)
        ring = raw[:].rearrange("p a k n -> p (a k) n")
        sw_hi = sb("sw_hi", [P, 3, KD, D], f32r)
        sw_lo = sb("sw_lo", [P, 3, KD, D], f32r)
        gw_hi = sb("gw_hi", [P, KD, D], f32r)
        gw_lo = sb("gw_lo", [P, KD, D], f32r)
        scan = sb("scan", [P, TILES * EC], fp32)
        work = sb("work", [P, TILES * EC], fp32)
        onehot = sb("onehot", [P, TILES * EC], bf16)
        rec = sb("rec", [P, 4, EC], fp32)
        slot_tile = sb("slot_tile", [P, EC], fp32)
        slot_lane = sb("slot_lane", [P, EC], fp32)
        ends = sb("ends", [P, 6, TILES], fp32)
        ends_i = sb("ends_i", [P, TILES], i32)
        quad_tab = sb("quad_tab", [P, TILES + 1], i32)
        rounds = sb("rounds", [P, 1], i32)
        row_oh = sb("row_oh", [P, QUAD - 1, P], f32r)
        row_w = sb("row_w", [P, P], fp32)
        scratch = sb("scratch", [P, 8, EC], fp32)
        src_i, dst_i, block_i, lane_i = (scratch[:, j].bitcast(i32) for j in range(4))
        pos_i, tile_i, slot_i = (scratch[:, j].bitcast(i32) for j in range(4, 7))
        pos_f = scratch[:, 7]
        ew_f, block_f = (scratch[:, j] for j in range(5, 7))
        rows2 = scratch[:].rearrange("p (a s b) k -> p a s (b k)", a=2, s=2)
        hwb, xn = rows2[:, 0], rows2[:, 1]
        tok_sorted = rec[:, 0, 0:MAX_TILES].bitcast(u32)
        texp_row = rec[0:1, 1, 0:P].bitcast(i32)
        sdst = scan[:, 1024:1024 + CHUNKS].bitcast(u32)
        slane = scan[:, 1024 + CHUNKS:1024 + 2 * CHUNKS]
        sew = scan[:, 1024 + 2 * CHUNKS:1024 + 3 * CHUNKS]
        logits = scan[:, 2048:2048 + TILES * EXPERTS].rearrange("p (t e) -> p t e", t=TILES)
        iota_i = scan[:, 0:CHUNKS].bitcast(i32)
        gw_hi_flat, gw_lo_flat = (t[:].rearrange("p k n -> p (k n)") for t in (gw_hi, gw_lo))
        lane_oh = gw_hi_flat.rearrange("p (s c f n) -> p s c f n", s=2, c=2, f=4)
        tile_oh = gw_lo_flat[:, 0:4 * CHUNKS].rearrange("p (s c n) -> p s c n", s=2, c=2)
        g_hi, g_lo = gw_hi, gw_lo
        ht_hi, ht_lo = gw_hi, gw_lo
        route = ring[:, HALF:RING].rearrange("p r n -> p (r n)")
        top8 = route[:, 0:128].rearrange("p (t j) -> p t j", t=TILES)
        idx8 = route[:, 128:256].bitcast(u32).rearrange("p (t j) -> p t j", t=TILES)
        r_small = route[:, 256:576].rearrange("p (j k t) -> p j k t", j=10, k=TOPK)
        r_int = route[:, 576:672].bitcast(i32).rearrange("p (j k t) -> p j k t", j=3, k=TOPK)
        x_small = route[:, 1024:1536].rearrange("p (j e) -> p j e", j=8)
        x_int = route[:, 1536:1600].bitcast(i32)
        stage = sb("stage", [P, RING], u32)
        bias_hi = sb("bias_hi", [1, D], f32r)
        bias_lo = sb("bias_lo", [1, D], f32r)
        gt_hi = sb("gt_hi", [P, KD, EXPERTS], f32r)
        gt_lo = sb("gt_lo", [P, KD, EXPERTS], f32r)
        xt_hi = sb("xt_hi", [P, 2, KD, P], f32r)
        ew_r = xt_hi[:, 0, 0:EC // P, :].rearrange("p k n -> p (k n)")
        xt_lo = sb("xt_lo", [P, 2, KD, P], f32r)
        sht_hi, sht_lo = xt_hi[:, 1], xt_lo[:, 1]
        hid = sb("hid", [P, 2, D], fp32)
        scatter_rec = work[:, 2048:2048 + 2 * SCATTER * 4].rearrange("p (s c f) -> p s c f", s=2, f=4)
        slot_index = work[:, 3072:3072 + EC].bitcast(u32)
        scattered = work[:, 0:CHUNKS * 4].rearrange("p (c f) -> p c f", f=4)
        lane_plain = hid[:, 0].rearrange("p (s c n) -> p s c n", s=2, c=2)
        gate_f = hid[0:EXPERTS, 0]
        bias_f = hid[0:1, 1]
        stats = sb("stats", [P, TILES, 6], fp32)
        mv = sb("mv", [P, TILES, 2], fp32)
        rstd = sb("rstd", [P, TILES], fp32)
        newton = sb("newton", [P, 4, TILES], fp32)
        comb_idx = sb("comb_idx", [P, TILES, TOPK], u32)
        texp_f = sb("texp_f", [P, 2], fp32)
        groups = sb("groups", [P, 1], i32)
        ident = sb("ident", [P, P], fp32)
        before_neg = sb("before_neg", [P, P], bf16)
        ones_b = sb("ones_b", [P, P], bf16)
        one_r = sb("one_r", [1, P], f32r)
        iota_f = sb("iota_f", [P, CHUNKS], fp32)
        tok_i = sb("tok_i", [P, TILES], i32)
        tok_f = sb("tok_f", [P, TILES], fp32)
        zeros = sb("zeros", [P, D], bf16)

        yg = [ring[:, 0:HALF], work[:].rearrange("p (r n) -> p r n", n=D)]
        sw_part = 3 * KD * D // TILES
        sw_raw_flat = raw[:, 1:4].rearrange("p a k n -> p (a k n)")
        sw_hi_flat, sw_lo_flat = (t[:].rearrange("p a k n -> p (a k n)") for t in (sw_hi, sw_lo))
        w_raw = [t[:, 0:KD * 2 * H + KH * D] for t in (scan, work)]
        w13_raw = [w[:, 0:KD * 2 * H].rearrange("p (m k n) -> p m k n", m=2, k=KD) for w in w_raw]
        w2_raw = [w[:, KD * 2 * H:].rearrange("p (k n) -> p k n", k=KH) for w in w_raw]

        def split_views(t):
            flat = t[:].rearrange("p a k n -> p (a k n)")
            n = KD * 2 * H + KH * D
            return ([flat[:, s * n:s * n + KD * 2 * H] for s in range(2)],
                    [flat[:, s * n + KD * 2 * H:(s + 1) * n] for s in range(2)])

        w13_hi, w2_hi = split_views(sw_hi)
        w13_lo, w2_lo = split_views(sw_lo)

        psum = ctx.enter_context(nc.psum_tensor("psum", [P, 8, 512], fp32))

        edges_in, x_in, gw_in, w_in = sem("edges_in"), sem("x_in"), sem("gw_in"), sem("w_in")
        consts, pool_steps = sem("consts"), sem("pool_steps")
        w_hi_done, w_split, sw_hi_done = sem("w_hi_done"), sem("w_split"), sem("sw_hi_done")
        counts_used = sem("counts_used")
        slots_ready, scatter_staged, table_zeroed, table_in = (
            sem("slots_ready"), sem("scatter_staged"), sem("table_zeroed"), sem("table_in"))
        scatter_done = [sem(f"scatter_done{s}") for s in range(2)]
        gate_t = sem("gate_t")
        onehot_ready, totals_ready, scan_done, prefix_ready = (
            sem("onehot_ready"), sem("totals_ready"), sem("scan_done"), sem("prefix_ready"))
        xn_ready, xt_ready, xth_ready, xtl_ready, hw_ready, hw_evac = (
            sem("xn_ready"), sem("xt_ready"), sem("xth_ready"), sem("xtl_ready"), sem("hw_ready"), sem("hw_evac"))
        hw_stored = [sem(f"hw_stored{s}") for s in range(2)]
        sort_plain, sort_dve, sort_act, sort_used, sorted_ready = (
            sem("sort_plain"), sem("sort_dve"), sem("sort_act"), sem("sort_used"), sem("sorted_ready"))
        dve_rank, dve_ln, dve_block, dve_route = (
            sem("dve_rank"), sem("dve_ln"), sem("dve_block"), sem("dve_route"))
        staged, xstaged = sem("staged"), sem("xstaged")
        gathered = [sem(f"gathered{j}") for j in range(QUADS_RING)]
        ghi_ready, split_ready, agg_used, agg_ready, x1_done = (
            sem("ghi_ready"), sem("split_ready"), sem("agg_used"), sem("agg_ready"), sem("x1_done"))
        xn2_ready, xn2_stored = sem("xn2_ready"), sem("xn2_stored")
        t2_ready, x2h_ready, x2l_ready, h_ready, silu_ready, hs_ready = (
            sem("t2_ready"), sem("x2h_ready"), sem("x2l_ready"), sem("h_ready"), sem("silu_ready"), sem("hs_ready"))
        logits_ready = sem("logits_ready")
        hT_ready, hTh_ready, hTl_ready, y_ready, shared_done = (
            sem("hT_ready"), sem("hTh_ready"), sem("hTl_ready"), sem("y_ready"), sem("shared_done"))
        top_ready, sig_ready, pairs_oh, rtot, rpre, texp_c, texp_t, experts_known, tables = (
            sem("top_ready"), sem("sig_ready"), sem("pairs_oh"), sem("rtot"), sem("rpre"),
            sem("texp_c"), sem("texp_t"), sem("experts_known"), sem("tables"))
        tsort_ready, tsort_used = sem("tsort_ready"), sem("tsort_used")
        w13_loaded = [sem(f"w13_loaded{s}") for s in range(2)]
        w2_loaded = [sem(f"w2_loaded{s}") for s in range(2)]
        xg_in = [sem(f"xg_in{s}") for s in range(2)]
        w13h, w13l, w2h, w2l = sem("w13h"), sem("w13l"), sem("w2h"), sem("w2l")
        ext_ready, exh_ready, exl_ready, h13_ready, sil_ready, eh_ready = (
            sem("ext_ready"), sem("exh_ready"), sem("exl_ready"), sem("h13_ready"), sem("sil_ready"), sem("eh_ready"))
        eht_ready, ehth_ready, ehtl_ready, ey_ready, ey_evac = (
            sem("eht_ready"), sem("ehth_ready"), sem("ehtl_ready"), sem("ey_ready"), sem("ey_evac"))
        ys_stored = [sem(f"ys_stored{s}") for s in range(2)]
        ys_zeroed = sem("ys_zeroed")
        cstaged, held = sem("cstaged"), sem("held")
        yg_in = [sem(f"yg_in{s}") for s in range(RING)]
        combined, out_stored, comb_steps = sem("combined"), sem("out_stored"), sem("comb_steps")

        def hold(engine):
            engine.sem_inc(held, 1)

        def mm3(pe, o, a_hi, a_lo, b_hi, b_lo, first, last):
            pe.matmul(o, a_hi, b_hi, start=first, stop=False)
            pe.matmul(o, a_lo, b_hi, start=False, stop=False)
            return pe.matmul(o, a_hi, b_lo, start=False, stop=last)

        def rows4(ap, k, n):
            return ap.rearrange("p (m n) -> p n m", n=n)[:, k, :]

        def within(b, lag):
            return not isinstance(b, int) or lag <= b < TILES + lag

        def blocks(engine, aggregate, boundary, routing=None):
            for b in range(DRAIN):
                aggregate(b)
                boundary(b)
            with engine.Fori(DRAIN, TILES) as b:
                aggregate(b)
                boundary(b)
            for b in range(TILES, TILES + DRAIN - 1):
                boundary(b)
                if routing and b == TILES + 1:
                    routing()

        block = ctx.enter_context(nc.Block())

        @block.sync
        def _(sp):
            sp.dma_start(src_i, src.rearrange("(p k) -> p k", p=P)).then_inc(edges_in, 16)
            sp.dma_start(dst_i, dst.rearrange("(p k) -> p k", p=P)).then_inc(edges_in, 16)
            sp.dma_start(ew_f, edge_weight.rearrange("(p k) -> p k", p=P)).then_inc(edges_in, 16)
            sp.dma_start(acc[:], x.rearrange("(t p) d -> p t d", p=P)).then_inc(x_in, 16)
            for m, w in enumerate((gnn_w, sw1, sw3, sw2)):
                sp.dma_start(raw[:, m], w.rearrange("(p k) n -> p k n", p=P)).then_inc(w_in if m else gw_in, 16)
            sp.dma_start(gate_f, gate_w).then_inc(w_in, 16)
            sp.dma_start(bias_f, gnn_bias.rearrange("(a d) -> a d", a=1)).then_inc(w_in, 16)
            sp.wait_ge(consts, 1)
            zero_row = zeros[:].bitcast(fp32)
            sp.dma_start(sort_dram.rearrange("(p a n) f -> p a (n f)", p=P, n=D // 8),
                         zero_row.unsqueeze(1).to_broadcast([P, CHUNKS * 8 // D, D // 2])).then_inc(table_zeroed, 16)
            zero_part = 16
            zero_sems = [ys_zeroed] * (2 * MAX_TILES // zero_part - 2) + ys_stored
            sp.wait_ge(hw_ready, TILES)
            for q, zeroed in enumerate(zero_sems):
                sp.wait_ge(scatter_staged, q + 7)
                sp.dma_start(ys_dram.rearrange("(p r) (h n) -> p (r h) n", p=P, h=2)[:, zero_part * q:zero_part * (q + 1)],
                             zero_row.unsqueeze(1).to_broadcast([P, zero_part, D // 2])).then_inc(zeroed, 16)
            for s in range(2):
                sp.wait_ge(scatter_done[s], 16 * SCATTERED // 2)
            sp.dma_start(scattered, sort_dram.rearrange("(p c) f -> p c f", p=P)).then_inc(table_in, 16)
            with sp.Fori(0, TILES) as t:
                sp.wait_ge(xn2_ready, t + 1)
                sp.dma_start(xn_dram[bass.ds(t * P, P), :], xn[:, 0]).then_inc(xn2_stored, 16)
            sp.wait_ge(experts_known, 1)
            middle = sp.value_load(groups[0:1, 0:1], min_val=1, max_val=MAX_TILES // 2 - 2)

            def expert(b, c):
                return bass.ds(sp.value_load(texp_row[0:1, bass.ds(b + c, 1)], min_val=0, max_val=EXPERTS - 1), 1)

            def load13(b, c):
                s, e = c % 2, expert(b, c)
                sp.wait_ge(w13l, b + (c + 1))
                for m, w in enumerate((w1, w3)):
                    sp.dma_start(w13_raw[s][:, m], w[e].rearrange("a (p k) n -> p (a k) n", p=P)).then_inc(w13_loaded[s], 16)

            def load2(b, c):
                s, e = c % 2, expert(b, c)
                sp.wait_ge(w2l, b + (c + 1))
                sp.dma_start(w2_raw[s], w2[e].rearrange("a (p k) n -> p (a k) n", p=P)).then_inc(w2_loaded[s], 16)

            load13(0, 0)
            with sp.Fori(0, middle + 1) as g:
                for c in range(1, 3):
                    load13(2 * g, c)
                    load2(2 * g, c - 1)
            rest = 2 * middle + 2
            load13(rest, 1)
            load2(rest, 0)
            load2(rest, 1)
            with sp.Fori(0, TILES) as t:
                sp.wait_ge(combined, t + (1 + RING // TOPK))
                sp.dma_start(out[bass.ds(t * P, P), :], acc[:, bass.ds(t, 1), :]).then_inc(out_stored, 16)
            sp.wait_ge(out_stored, 16 * TILES)

        @block.gpsimd
        def _(pool):
            st = Steps(pool, pool_steps)
            st.add(pool.memset(ident[:], 0.0))
            st.add(pool.memset(before_neg[:], -1.0))
            st.add(pool.iota(iota_i, [[1, CHUNKS]], base=0, channel_multiplier=0))
            st.add(pool.iota(tok_i[:], [[P, TILES]], base=0, channel_multiplier=1))
            st.wait()
            st.add(pool.affine_select(out=ident[:], in_=ident[:], compare_op=ALU.not_equal, fill=1.0,
                                      base=0, pattern=[[-1, P]], channel_multiplier=1))
            st.add(pool.affine_select(out=before_neg[:], in_=before_neg[:], compare_op=ALU.is_ge, fill=0.0,
                                      base=0, pattern=[[-1, P]], channel_multiplier=1))
            st.add(pool.tensor_copy(iota_f[:], iota_i))
            st.add(pool.tensor_copy(tok_f[:], tok_i[:]))
            st.add(pool.memset(ones_b[:], 1.0))
            st.add(pool.memset(zeros[:], 0.0))
            st.wait()
            pool.sem_inc(consts, 1)
            pool.wait_ge(slots_ready, 1)
            pool.wait_ge(table_zeroed, 16)

            def scatter(b, c):
                s = c % 2
                if within(b, 2):
                    pool.wait_ge(scatter_done[s], (b - 2) * (8 * SCATTER) + (c - s + 2) * (8 * SCATTER))
                    hold(pool)
                first = SCATTER * b + (SORT_COLS + SCATTER * c)
                pool.tensor_copy(stage[:, SCATTER * s:SCATTER * (s + 1)], slot_index[:, bass.ds(first, SCATTER)])
                pool.tensor_copy(scatter_rec[:, s], rec[:, :, bass.ds(first, SCATTER)].rearrange("p f c -> p c f")
                                 ).then_inc(scatter_staged, 1)
                pool.wait_ge(scatter_staged, b + (c + 1))
                hold(pool)
                for j in range(SCATTER):
                    pool.indirect_dma_start(sort_dram, bass.IndirectOffsetOnAxis(
                        stage[:, SCATTER * s + j:SCATTER * s + j + 1], 0), scatter_rec[:, s, j], None
                                            ).then_inc(scatter_done[s], 16)

            scatter(0, 0)
            scatter(0, 1)
            with pool.Fori(1, SCATTERED // SCATTER // 2) as i:
                scatter(2 * i, 0)
                scatter(2 * i, 1)
            for s in range(2):
                pool.wait_ge(hw_stored[s], 16 * (TILES // 2))
            pool.wait_ge(sort_dve, 1)
            for j in range(1, QUADS_RING):
                pool.indirect_dma_start(ring[:, QUAD * j], None, hw_dram,
                                        bass.IndirectOffsetOnAxis(tok_i[:, 0:1].bitcast(u32), 0)).then_inc(gathered[j], 16)
            for j in range(1, QUADS_RING):
                pool.wait_ge(gathered[j], 16)
            n_rounds = pool.value_load(rounds[0:1, 0:1], min_val=1, max_val=CHUNKS // RING)
            pool.wait_ge(sorted_ready, 1)
            with pool.Fori(0, n_rounds) as i:
                for j in range(QUADS_RING):
                    pool.wait_ge(agg_used, RING * i + QUAD * (j + 1))
                    pool.tensor_copy(stage[:, QUAD * j:QUAD * (j + 1)], sdst[:, bass.ds(RING * i + QUAD * j, QUAD)]
                                     ).then_inc(staged, 1)
                    pool.wait_ge(staged, QUADS_RING * i + (j + 1))
                    hold(pool)
                    for r in range(QUAD * j, QUAD * (j + 1)):
                        pool.indirect_dma_start(ring[:, r], None, hw_dram, bass.IndirectOffsetOnAxis(stage[:, r:r + 1], 0)
                                                ).then_inc(gathered[j], 16)
            pool.wait_ge(tables, 1)
            pool.wait_ge(xn2_stored, 16 * TILES)
            middle = pool.value_load(groups[0:1, 0:1], min_val=1, max_val=MAX_TILES // 2 - 2)
            with pool.Fori(0, middle + 2) as g:
                for s in range(2):
                    pool.wait_ge(ext_ready, 2 * g + s + 1)
                    pool.tensor_copy(stage[:, s:s + 1], tok_sorted[:, bass.ds(2 * g + s, 1)]).then_inc(xstaged, 1)
                    pool.wait_ge(xstaged, 2 * g + s + 1)
                    hold(pool)
                    pool.indirect_dma_start(hwb[:, s], None, xn_dram,
                                            bass.IndirectOffsetOnAxis(stage[:, s:s + 1], 0)).then_inc(xg_in[s], 16)
            for s in range(2):
                pool.wait_ge(ys_stored[s], 16 * middle + 48)
            hold(pool)
            with pool.Fori(0, TILES * TOPK // RING) as i:
                for h in range(2):
                    first = RING * i + HALF * h
                    pool.wait_ge(combined, (RING // TOPK) * i + (h + 1) * (HALF // TOPK))
                    pool.tensor_copy(stage[:, HALF * h:HALF * (h + 1)],
                                     comb_idx[:].rearrange("p t k -> p (t k)")[:, bass.ds(first, HALF)]).then_inc(cstaged, 1)
                    pool.wait_ge(cstaged, 2 * i + h + 1)
                    hold(pool)
                    for r in range(HALF):
                        pool.indirect_dma_start(yg[h][:, r], None, ys_dram,
                                                bass.IndirectOffsetOnAxis(stage[:, HALF * h + r:HALF * h + r + 1], 0)
                                                ).then_inc(yg_in[HALF * h + r], 16)

        @block.tensor
        def _(pe):
            pe.sem_inc(sort_used, 4)
            pe.sem_inc(agg_used, RING)
            pe.sem_inc(tsort_used, 2 * TOPK)
            pe.sem_inc(ext_ready, 2)
            pe.sem_inc(h13_ready, 2)
            pe.sem_inc(ey_ready, 2)
            pe.wait_ge(consts, 1)
            pe.wait_ge(onehot_ready, 1)
            for b in range(8):
                pe.matmul(psum[:, b], ones_b[:], onehot[:, 512 * b:512 * b + 512], start=True, stop=True
                          ).then_inc(totals_ready, 1)
            for b in range(8):
                pe.wait_ge(scan_done, b + 1)
                pe.matmul(psum[:, b], before_neg[:], onehot[:, 512 * b:512 * b + 512], start=True, stop=True
                          ).then_inc(prefix_ready, 1)
            pe.wait_ge(counts_used, 1)
            pe.wait_ge(w_in, 80)
            for k in range(KD):
                last = pe.transpose(psum[:, 3, EXPERTS * k:EXPERTS * (k + 1)], rows4(gate_f, k, KD),
                                    ident[0:EXPERTS, 0:EXPERTS])
            last.then_inc(gate_t, 1)

            def x_transpose1(b, c):
                s = c % 2
                pe.wait_ge(xn_ready, b + (c + 1))
                for k in range(KD):
                    last = pe.transpose(psum[:, 4 + s, P * k:P * (k + 1)], rows4(xn[:, s], k, KD), ident[:])
                last.then_inc(xt_ready, 1)

            def product(b, s, ahead=True):
                if ahead:
                    x_transpose1(b, s + 1)
                pe.wait_ge(xtl_ready, b + (s + 1))
                pe.wait_ge(hw_evac, b + (s + 1))
                for k in range(KD):
                    last = mm3(pe, psum[:, 6 + s], xt_hi[:, s, k], xt_lo[:, s, k], gw_hi[:, k], gw_lo[:, k],
                               k == 0, k == KD - 1)
                last.then_inc(hw_ready, 1)

            x_transpose1(0, 0)
            pe.wait_ge(w_split, 1)
            with pe.Fori(0, TILES // 2 - 1) as i:
                product(2 * i, 0)
                product(2 * i, 1)
            product(TILES - 2, 0)
            product(TILES - 2, 1, ahead=False)
            for f in range(4):
                pe.matmul(psum[:, f, 0:CHUNKS], zeros[:, 0:P], zeros[:, 0:CHUNKS], start=True, stop=True)
            with pe.Fori(0, SORT_COLS // 4) as i:
                for s in range(2):
                    pe.wait_ge(sort_dve, 2 * i + s + 1)
                    for f in range(4):
                        if f == DVE_FIELDS:
                            pe.wait_ge(sort_act, 2 * i + s + 1)
                        for c in range(2):
                            last = pe.matmul(psum[:, f, 0:CHUNKS], lane_oh[:, s, c, f], tile_oh[:, s, c],
                                             start=False, stop=True, skip_group_check=True)
                    last.then_inc(sort_used, 2)
            pe.wait_ge(sorted_ready, 1)

            def boundary(b):
                if within(b, 1):
                    pe.wait_ge(x2l_ready, b)
                    if within(b, 2):
                        pe.wait_ge(hs_ready, b - 1)
                    for k in range(KD):
                        mm3(pe, psum[:, 2, 0:EXPERTS], xt_hi[:, 0, k], xt_lo[:, 0, k], gt_hi[:, k], gt_lo[:, k],
                            k == 0, k == KD - 1)
                    for m in range(2):
                        for k in range(KD):
                            last = mm3(pe, psum[:, 3 + m], xt_hi[:, 0, k], xt_lo[:, 0, k],
                                       sw_hi[:, m, k], sw_lo[:, m, k], k == 0, k == KD - 1)
                    last.then_inc(h_ready, 1)
                if within(b, 3):
                    pe.wait_ge(hTl_ready, b - 2)
                    if within(b, 4):
                        pe.wait_ge(shared_done, b - 3)
                    for k in range(KD):
                        last = mm3(pe, psum[:, 6], sht_hi[:, k], sht_lo[:, k], sw_hi[:, 2, k], sw_lo[:, 2, k],
                                   k == 0, k == KD - 1)
                    last.then_inc(y_ready, 1)
                if within(b, 2):
                    pe.wait_ge(hs_ready, b - 1)
                    for k in range(KD):
                        last = pe.transpose(psum[:, 5, P * k:P * (k + 1)], rows4(hid[:, 1], k, KD), ident[:])
                    last.then_inc(hT_ready, 1)
                if within(b, 0):
                    pe.wait_ge(xn2_ready, b + 1)
                    for k in range(KD):
                        last = pe.transpose(psum[:, 1, P * k:P * (k + 1)], rows4(xn[:, 0], k, KD), ident[:])
                    last.then_inc(t2_ready, 1)

            def aggregate(b):
                first = pe.value_load(quad_tab[0:1, bass.ds(b, 1)], min_val=0, max_val=QUADS)
                end = pe.value_load(quad_tab[0:1, bass.ds(b + 1, 1)], min_val=0, max_val=QUADS)
                if within(b, 1):
                    pe.wait_ge(x1_done, b)
                pe.matmul(psum[:, 0], one_r[:], bias_hi[:], start=True, stop=True)
                with pe.Fori(first, end) as q:
                    for s in range(QUAD - 1):
                        pe.wait_ge(split_ready, QUAD * q + (s + 1))
                        pe.matmul(psum[:, 0], row_oh[:, s], g_hi[:, s], start=False, stop=True, skip_group_check=True)
                        pe.matmul(psum[:, 0], row_oh[:, s], g_lo[:, s], start=False, stop=True, skip_group_check=True
                                  ).then_inc(agg_used, 1)
                    pe.wait_ge(split_ready, QUAD * q + QUAD)
                    pe.matmul(psum[:, 0], row_w[:], ring[:, bass.ds((q % QUADS_RING) * QUAD + QUAD - 1, 1), :],
                              start=False, stop=True, skip_group_check=True).then_inc(agg_used, 1)
                pe.matmul(psum[:, 0], one_r[:], bias_lo[:], start=False, stop=True, skip_group_check=True
                          ).then_inc(agg_ready, 1)

            def count_pairs():
                pe.wait_ge(pairs_oh, 1)
                for b in range(2):
                    last = pe.matmul(psum[:, b], ones_b[:], onehot[:, 512 * b:512 * b + 512], start=True, stop=True)
                last.then_inc(rtot, 1)
                for b in range(2):
                    last = pe.matmul(psum[:, 2 + b], before_neg[:], onehot[:, 512 * b:512 * b + 512],
                                     start=True, stop=True)
                last.then_inc(rpre, 1)

            blocks(pe, aggregate, boundary, count_pairs)
            pe.wait_ge(texp_c, 1)
            pe.matmul(psum[0:1, 5, 0:P], texp_f[:, 1:2], ident[:], start=True, stop=True).then_inc(texp_t, 1)
            pe.matmul(psum[:, 4, 0:MAX_TILES], zeros[:, 0:P], zeros[:, 0:MAX_TILES], start=True, stop=True)
            with pe.Fori(0, TILES // 2) as i:
                for j in range(2):
                    for k in range(TOPK):
                        pe.wait_ge(tsort_ready, 2 * TOPK * i + (TOPK * j + k + 1))
                        pe.matmul(psum[:, 4, 0:MAX_TILES], lane_oh[:, j, k, 0], tile_oh[:, j, k, 0:MAX_TILES],
                                  start=False, stop=True, skip_group_check=True).then_inc(tsort_used, 1)
            pe.wait_ge(tables, 1)
            middle = pe.value_load(groups[0:1, 0:1], min_val=1, max_val=MAX_TILES // 2 - 2)

            def x_transpose(b, c):
                s = c % 2
                pe.wait_ge(xg_in[s], b * 8 + (c - s) * 8 + 16)
                for k in range(KD):
                    last = pe.transpose(psum[:, s, P * k:P * (k + 1)], rows4(hwb[:, s], k, KD), ident[:])
                last.then_inc(ext_ready, 1)

            def up(b, c):
                s = c % 2
                pe.wait_ge(exl_ready, b + (c + 1))
                pe.wait_ge(w13l, b + (c + 3))
                for k in range(KD):
                    last = mm3(pe, psum[:, 2 + s], xt_hi[:, s, k], xt_lo[:, s, k],
                               w13_hi[s].rearrange("p (m k n) -> p m k n", m=2, k=KD)[:, :, k],
                               w13_lo[s].rearrange("p (m k n) -> p m k n", m=2, k=KD)[:, :, k],
                               k == 0, k == KD - 1)
                last.then_inc(h13_ready, 1)

            def h_transpose(b, c):
                s = c % 2
                pe.wait_ge(eh_ready, b + (c + 1))
                for k in range(KH):
                    last = pe.transpose(psum[:, 4 + s, P * k:P * (k + 1)], rows4(hid[:, s, H:2 * H], k, KH), ident[:])
                last.then_inc(eht_ready, 1)

            def down(b, c):
                s = c % 2
                pe.wait_ge(ehtl_ready, b + (c + 1))
                pe.wait_ge(w2l, b + (c + 3))
                pe.wait_ge(ey_evac, b + (c + 1))
                for k in range(KH):
                    last = mm3(pe, psum[:, 6 + s], ht_hi[:, 2 * s + k, 0:P], ht_lo[:, 2 * s + k, 0:P],
                               w2_hi[s].rearrange("p (k n) -> p k n", k=KH)[:, k],
                               w2_lo[s].rearrange("p (k n) -> p k n", k=KH)[:, k], k == 0, k == KH - 1)
                last.then_inc(ey_ready, 1)

            def step(b, c, x_ahead=True, before=True):
                if x_ahead:
                    x_transpose(b, c + 1)
                up(b, c)
                if before:
                    down(b, c - 1)
                h_transpose(b, c)

            x_transpose(0, 0)
            step(0, 0, before=False)
            with pe.Fori(0, middle) as g:
                step(2 * g, 1)
                step(2 * g, 2)
            rest = 2 * middle
            step(rest, 1)
            step(rest, 2)
            step(rest, 3, x_ahead=False)
            down(rest, 3)

        @block.scalar
        def _(act):
            act.sem_inc(ey_evac, 2)
            act.sem_inc(hw_evac, 2)
            act.wait_ge(consts, 1)
            nc.scalar.copy(one_r[:], ones_b[0:1, :]).then_inc(w_hi_done, 1)
            act.wait_ge(gw_in, 16)
            nc.scalar.copy(gw_hi[:], raw[:, 0]).then_inc(w_hi_done, 1)
            act.wait_ge(w_in, 80)
            nc.scalar.copy(bias_hi[:], bias_f).then_inc(w_hi_done, 1)
            act.wait_ge(gate_t, 1)
            nc.scalar.copy(gt_hi[:], psum[:, 3, 0:KD * EXPERTS].rearrange("p (k e) -> p k e", k=KD)
                           ).then_inc(w_hi_done, 1)

            def x_high1(b, c):
                s = c % 2
                act.wait_ge(xt_ready, b + (c + 1))
                nc.scalar.copy(xt_hi[:, s], psum[:, 4 + s].rearrange("p (k n) -> p k n", k=KD)).then_inc(xth_ready, 1)

            def product(b, s, ahead=True):
                if ahead:
                    x_high1(b, s + 1)
                part = bass.ds(sw_part * b + sw_part * s, sw_part)
                nc.scalar.copy(sw_hi_flat[:, part], sw_raw_flat[:, part]).then_inc(sw_hi_done, 1)
                act.wait_ge(hw_ready, b + (s + 1))
                if within(b, 1):
                    act.wait_ge(hw_stored[s], 8 * b)
                nc.scalar.copy(hwb[:, s], psum[:, 6 + s]).then_inc(hw_evac, 1)
                act.wait_ge(hw_evac, b + (s + 3))
                act.dma_start(hw_dram[bass.ds(b * P + s * P, P), :], hwb[:, s]).then_inc(hw_stored[s], 16)

            x_high1(0, 0)
            product(0, 0)
            product(0, 1)
            with act.Fori(1, TILES // 2 - 1) as i:
                product(2 * i, 0)
                product(2 * i, 1)
            product(TILES - 2, 0)
            product(TILES - 2, 1, ahead=False)
            with act.Fori(0, SORT_COLS // 4) as i:
                for s in range(2):
                    act.wait_ge(sort_plain, 2 * i + s + 1)
                    for c in range(2):
                        for f in range(DVE_FIELDS, 4):
                            last = nc.scalar.activation(lane_oh[:, s, c, f], lane_plain[:, s, c], ACT.Copy,
                                                        scale=rec[:, f, bass.ds(4 * i + 2 * s + c, 1)])
                    last.then_inc(sort_act, 1)
            act.wait_ge(sorted_ready, 1)

            def aggregate(b):
                first = act.value_load(quad_tab[0:1, bass.ds(b, 1)], min_val=0, max_val=QUADS)
                end = act.value_load(quad_tab[0:1, bass.ds(b + 1, 1)], min_val=0, max_val=QUADS)
                with act.Fori(first, end) as q:
                    act.wait_ge(gathered[0], (q // QUADS_RING) * (16 * QUAD) + 16 * QUAD)
                    for j in range(1, QUADS_RING):
                        act.wait_ge(gathered[j], ((q + (QUADS_RING - j)) // QUADS_RING) * (16 * QUAD) + 16)
                    for s in range(QUAD - 1):
                        act.wait_ge(agg_used, QUAD * q + (RING - QUAD + s + 1))
                        nc.scalar.activation(g_hi[:, s], ring[:, bass.ds((q % QUADS_RING) * QUAD + s, 1), :], ACT.Copy,
                                             scale=sew[:, bass.ds(QUAD * q + s, 1)]).then_inc(ghi_ready, 1)

            def boundary(b):
                if within(b, 1):
                    act.wait_ge(t2_ready, b)
                    if within(b, 2):
                        act.wait_ge(h_ready, b - 1)
                    nc.scalar.copy(xt_hi[:, 0], psum[:, 1].rearrange("p (k n) -> p k n", k=KD)).then_inc(x2h_ready, 1)
                if within(b, 2):
                    act.wait_ge(h_ready, b - 1)
                    if within(b, 3):
                        act.wait_ge(hs_ready, b - 2)
                    nc.scalar.activation(hid[:, 0], psum[:, 3], ACT.Silu).then_inc(silu_ready, 1)
                    nc.scalar.copy(logits[:, bass.ds(b - 2, 1), :], psum[:, 2, 0:EXPERTS]).then_inc(logits_ready, 1)
                if within(b, 3):
                    act.wait_ge(hT_ready, b - 2)
                    if within(b, 4):
                        act.wait_ge(y_ready, b - 3)
                    nc.scalar.copy(sht_hi, psum[:, 5].rearrange("p (k n) -> p k n", k=KD)).then_inc(hTh_ready, 1)

            blocks(act, aggregate, boundary)
            act.wait_ge(top_ready, 1)
            nc.scalar.activation(r_small[:, 0], top8[:, :, 0:TOPK].rearrange("p t k -> p k t"), ACT.Sigmoid
                                 ).then_inc(sig_ready, 1)
            act.wait_ge(experts_known, 1)
            middle = act.value_load(groups[0:1, 0:1], min_val=1, max_val=MAX_TILES // 2 - 2)

            def split13(b, c):
                s = c % 2
                act.wait_ge(w13_loaded[s], b * 16 + (c - s) * 16 + 32)
                act.wait_ge(h13_ready, b + (c + 1))
                nc.scalar.copy(w13_hi[s], w_raw[s][:, 0:KD * 2 * H]).then_inc(w13h, 1)

            def split2(b, c):
                s = c % 2
                act.wait_ge(w2_loaded[s], b * 8 + (c - s) * 8 + 16)
                act.wait_ge(ey_ready, b + (c + 1))
                nc.scalar.copy(w2_hi[s], w_raw[s][:, KD * 2 * H:]).then_inc(w2h, 1)

            def x_high(b, c):
                s = c % 2
                act.wait_ge(ext_ready, b + (c + 3))
                nc.scalar.copy(xt_hi[:, s], psum[:, s].rearrange("p (k n) -> p k n", k=KD)).then_inc(exh_ready, 1)

            def h_high(b, c):
                s = c % 2
                act.wait_ge(eht_ready, b + (c + 1))
                nc.scalar.copy(ht_hi[:, 2 * s:2 * s + 2, 0:P], psum[:, 4 + s, 0:H].rearrange("p (k n) -> p k n", k=KH)
                               ).then_inc(ehth_ready, 1)

            def silu(b, c):
                s = c % 2
                act.wait_ge(h13_ready, b + (c + 3))
                nc.scalar.activation(hid[:, s, 0:H], psum[:, 2 + s, 0:H], ACT.Silu).then_inc(sil_ready, 1)

            def store(b, c):
                s = c % 2
                act.wait_ge(ey_ready, b + (c + 3))
                act.wait_ge(ys_stored[s], b * 8 + (c - s) * 8 + 16)
                nc.scalar.copy(xn[:, s], psum[:, 6 + s]).then_inc(ey_evac, 1)
                act.wait_ge(ey_evac, b + (c + 3))
                act.dma_start(ys_dram[bass.ds(b * P + c * P, P), :], xn[:, s]).then_inc(ys_stored[s], 16)

            def step(b, c, before=True, ahead=2):
                if ahead >= 1:
                    x_high(b, c + 1)
                silu(b, c)
                if ahead == 2:
                    split13(b, c + 2)
                h_high(b, c)
                if before:
                    store(b, c - 1)
                if ahead >= 1:
                    split2(b, c + 1)

            act.wait_ge(ys_zeroed, 16 * (2 * MAX_TILES // 16 - 2))
            for s in range(2):
                act.wait_ge(ys_stored[s], 16)
            split13(0, 0)
            split13(0, 1)
            split2(0, 0)
            x_high(0, 0)
            step(0, 0, before=False)
            with act.Fori(0, middle) as g:
                step(2 * g, 1)
                step(2 * g, 2)
            rest = 2 * middle
            step(rest, 1)
            step(rest, 2, ahead=1)
            step(rest, 3, ahead=0)
            store(rest, 3)

        @block.vector
        def _(v):
            v.sem_inc(w13l, 2)
            v.sem_inc(w2l, 2)
            v.sem_inc(combined, RING // TOPK)

            def rsqrt(step, o, a, b, width):
                step(v.tensor_scalar(a[0], a[0], EPS, None, ALU.add))
                step.add(v.tensor_scalar(a[1], a[0], 0.25, None, ALU.mult))
                step.add(v.tensor_scalar(a[2], a[0], 0.0625, None, ALU.mult))
                step(v.tensor_scalar(b.bitcast(i32), a[0].bitcast(i32), 1, None, ALU.logical_shift_right))
                step(v.tensor_scalar(o.bitcast(i32), b.bitcast(i32), -1.0, float(RSQRT_GUESS), ALU.mult, ALU.add))
                for k in range(3):
                    if width == 1:
                        step(v.scalar_tensor_tensor(b, o, a[k], o, ALU.mult, ALU.mult))
                    else:
                        step(v.tensor_tensor(b, a[k], o, ALU.mult))
                        step(v.tensor_tensor(b, b, o, ALU.mult))
                    step(v.scalar_tensor_tensor(o, b, -3.0, o, ALU.add, ALU.mult))
                step(v.tensor_scalar(o, o, -0.125, None, ALU.mult))

            st = Steps(v, dve_rank)
            v.wait_ge(edges_in, 48)
            st.add(v.tensor_scalar(block_i, src_i, BLOCK_SHIFT, None, ALU.logical_shift_right))
            st.add(v.tensor_scalar(lane_i, src_i, P - 1, None, ALU.bitwise_and))
            st.add(v.tensor_copy(ew_r, ew_f))
            st.add(v.tensor_copy(rec[:, 0], dst_i))
            st.wait()
            st.add(v.tensor_copy(block_f, block_i))
            st.add(v.tensor_copy(rec[:, 1], lane_i))
            st.add(v.tensor_copy(rec[:, 2], ew_r.bitcast(fp32)))
            st.add(v.tensor_tensor(rec[:, 3], ew_f, ew_r.bitcast(fp32), ALU.subtract))
            st.wait()
            oh3 = onehot[:].rearrange("p (b k) -> p b k", b=TILES)
            for b in range(TILES):
                last = v.tensor_scalar(oh3[:, b], block_f, float(b), None, ALU.is_equal)
            last.then_inc(onehot_ready, 1)
            v.wait_ge(consts, 1)
            for b in range(8):
                v.wait_ge(totals_ready, b + 1)
                v.tensor_tensor_scan(scan[:, 512 * b:512 * b + 512], psum[:, b], zeros[:],
                                     0.0 if b == 0 else scan[:, 512 * b - 1:512 * b], ALU.add, ALU.add
                                     ).then_inc(scan_done, 1)
                v.wait_ge(scan_done, b + 1)
            scan3 = scan[:].rearrange("p (b k) -> p b k", b=TILES)
            last_count = scan3[:, :, EC - 1]
            cnt, n_quads, p_end, p_start, corr, tmp = (ends[:, j] for j in range(6))
            st.add(v.tensor_copy(cnt[:, 0:1], last_count[:, 0:1]))
            st.add(v.tensor_tensor(cnt[:, 1:], last_count[:, 1:], last_count[:, 0:TILES - 1], ALU.subtract))
            st.wait()
            st(v.tensor_scalar(tmp, cnt, float(QUAD * P - 1), None, ALU.add))
            st(v.tensor_copy(ends_i[:], tmp))
            st(v.tensor_scalar(ends_i[:], ends_i[:], QUAD_SHIFT, None, ALU.logical_shift_right))
            st(v.tensor_copy(n_quads, ends_i[:]))
            st(v.tensor_scalar(n_quads, n_quads, 1.0, None, ALU.max))
            st(v.tensor_tensor_scan(p_end, n_quads, zeros[:, 0:TILES], 0.0, ALU.add, ALU.add))
            st(v.tensor_tensor(p_start, p_end, n_quads, ALU.subtract))
            st.add(v.tensor_copy(quad_tab[:, 0:TILES], p_start))
            st(v.tensor_scalar(tmp[:, 0:1], p_end[:, TILES - 1:TILES], float(QUADS_RING - 1), None, ALU.add))
            st(v.tensor_copy(ends_i[:, 0:1], tmp[:, 0:1]))
            st(v.tensor_scalar(rounds[:], ends_i[:, 0:1], ROUND_SHIFT, None, ALU.logical_shift_right))
            st(v.tensor_scalar(quad_tab[:, TILES:], rounds[:], float(QUADS_RING), None, ALU.mult))
            st(v.tensor_tensor(corr, last_count, cnt, ALU.subtract))
            st(v.scalar_tensor_tensor(corr, p_start, float(QUAD * P), corr, ALU.mult, ALU.subtract))
            work3 = work[:].rearrange("p (b k) -> p b k", b=TILES)
            for b in range(TILES):
                v.wait_ge(prefix_ready, b // 2 + 1)
                st.add(v.scalar_tensor_tensor(work3[:, b], scan3[:, b], corr[:, b:b + 1],
                                              psum[:, b // 2, EC * (b % 2):EC * (b % 2 + 1)], ALU.add, ALU.add))
            st.wait()
            v.sem_inc(counts_used, 1)
            st(v.tensor_tensor(work[:], work[:], onehot[:], ALU.mult))
            st(v.tensor_reduce(pos_f, work3.rearrange("p b k -> p k b"), AX.X, ALU.add))
            st(v.tensor_copy(pos_i, pos_f))
            st.add(v.tensor_scalar(tile_i, pos_i, BLOCK_SHIFT, None, ALU.logical_shift_right))
            st(v.tensor_scalar(slot_i, pos_i, P - 1, None, ALU.bitwise_and))
            st.add(v.tensor_copy(slot_lane[:], slot_i))
            st(v.tensor_copy(slot_tile[:], tile_i))
            st(v.scalar_tensor_tensor(slot_index, slot_lane[:], float(CHUNKS), slot_tile[:], ALU.mult, ALU.add))
            v.sem_inc(slots_ready, 1)
            v.wait_ge(x_in, 16)
            sl = Steps(v, dve_ln)
            for t in range(TILES):
                sl.add(v.bn_stats(stats[:, t], acc[:, t]))
            sl.wait()
            for t in range(TILES):
                sl.add(v.bn_aggr(mv[:, t], stats[:, t]))
            sl.wait()
            sl(v.tensor_copy(newton[:, 0], mv[:, :, 1]))
            rsqrt(sl, rstd[:], [newton[:, k] for k in range(3)], newton[:, 3], TILES)

            def normalise(b, c):
                s = c % 2
                if not (isinstance(b, int) and b + c < 2):
                    v.wait_ge(xt_ready, b + (c - 1))
                v.tensor_scalar(xn[:, s], acc[:, bass.ds(b + c, 1), :],
                                mv[:, bass.ds(b + c, 1), 0:1].rearrange("p a b -> p (a b)"),
                                rstd[:, bass.ds(b + c, 1)], ALU.subtract, ALU.mult).then_inc(xn_ready, 1)

            def x_low1(b, c):
                s = c % 2
                v.wait_ge(xth_ready, b + (c + 1))
                v.tensor_tensor(xt_lo[:, s], psum[:, 4 + s].rearrange("p (k n) -> p k n", k=KD),
                                xt_hi[:, s].bitcast(fp32), ALU.subtract).then_inc(xtl_ready, 1)

            def product(b, s, ahead=2):
                if ahead >= 1:
                    x_low1(b, s + 1)
                if ahead == 2:
                    normalise(b, s + 2)
                part = bass.ds(sw_part * b + sw_part * s, sw_part)
                v.wait_ge(sw_hi_done, b + (s + 1))
                v.tensor_tensor(sw_lo_flat[:, part], sw_raw_flat[:, part], sw_hi_flat[:, part].bitcast(fp32), ALU.subtract)

            normalise(0, 0)
            normalise(0, 1)
            v.wait_ge(w_hi_done, 4)
            v.tensor_tensor(gw_lo[:], raw[:, 0], gw_hi[:].bitcast(fp32), ALU.subtract)
            v.tensor_tensor(bias_lo[:], bias_f, bias_hi[:].bitcast(fp32), ALU.subtract)
            v.tensor_tensor(gt_lo[:], psum[:, 3, 0:KD * EXPERTS].rearrange("p (k e) -> p k e", k=KD),
                            gt_hi[:].bitcast(fp32), ALU.subtract).then_inc(w_split, 1)
            x_low1(0, 0)
            with v.Fori(0, TILES // 2 - 1) as i:
                product(2 * i, 0)
                product(2 * i, 1)
            product(TILES - 2, 0, ahead=1)
            product(TILES - 2, 1, ahead=0)
            v.wait_ge(hw_ready, TILES)
            iota2 = iota_f[:, 0:P].unsqueeze(1).to_broadcast([P, 2, P])
            with v.Fori(0, SORT_COLS // 4) as i:
                for s in range(2):
                    first = 4 * i + 2 * s
                    v.wait_ge(sort_used, 4 * i + (2 * s + 2))
                    v.tensor_tensor(lane_plain[:, s], iota2,
                                    slot_lane[:, bass.ds(first, 2)].unsqueeze(2).to_broadcast([P, 2, P]),
                                    ALU.is_equal).then_inc(sort_plain, 1)
                    for c in range(2):
                        v.tensor_scalar(tile_oh[:, s, c], iota_f[:], slot_tile[:, bass.ds(first + c, 1)], None,
                                        ALU.is_equal)
                    v.wait_ge(sort_plain, 2 * i + s + 1)
                    n = DVE_FIELDS
                    v.tensor_tensor(lane_oh[:, s, :, 0:n], lane_plain[:, s].unsqueeze(2).to_broadcast([P, 2, n, P]),
                                    rec[:, 0:n, bass.ds(first, 2)].rearrange("p f c -> p c f").unsqueeze(3
                                        ).to_broadcast([P, 2, n, P]), ALU.mult).then_inc(sort_dve, 1)
            v.wait_ge(sort_used, SORT_COLS + 4)
            v.wait_ge(table_in, 16)
            sl.add(v.tensor_tensor(sdst, scattered[:, :, 0], psum[:, 0, 0:CHUNKS], ALU.add))
            sl.add(v.tensor_tensor(slane, scattered[:, :, 1], psum[:, 1, 0:CHUNKS], ALU.add))
            sl.add(v.tensor_tensor(sew, scattered[:, :, 2], psum[:, 2, 0:CHUNKS], ALU.add))
            sl(v.tensor_tensor(scattered[:, :, 3], scattered[:, :, 3], psum[:, 3, 0:CHUNKS], ALU.add))
            sl(v.tensor_tensor(sew, sew, scattered[:, :, 3], ALU.add))
            v.sem_inc(sorted_ready, 1)
            sk = Steps(v, dve_block)

            def row(b):
                return acc[:, bass.ds(b, 1), :].rearrange("p a n -> p (a n)")

            def aggregate(b):
                first = v.value_load(quad_tab[0:1, bass.ds(b, 1)], min_val=0, max_val=QUADS)
                end = v.value_load(quad_tab[0:1, bass.ds(b + 1, 1)], min_val=0, max_val=QUADS)
                with v.Fori(first, end) as q:
                    for s in range(QUAD - 1):
                        v.wait_ge(agg_used, QUAD * q + (RING - QUAD + s + 1))
                        v.tensor_scalar(row_oh[:, s], iota_f[:, 0:P], slane[:, bass.ds(QUAD * q + s, 1)], None,
                                        ALU.is_equal)
                        v.wait_ge(ghi_ready, (QUAD - 1) * q + (s + 1))
                        v.scalar_tensor_tensor(g_lo[:, s],
                                               ring[:, bass.ds((q % QUADS_RING) * QUAD + s, 1), :].rearrange("p a n -> p (a n)"),
                                               sew[:, bass.ds(QUAD * q + s, 1)], g_hi[:, s].bitcast(fp32),
                                               ALU.mult, ALU.subtract).then_inc(split_ready, 1)
                    v.wait_ge(agg_used, QUAD * q + RING)
                    v.tensor_scalar(row_w[:], iota_f[:, 0:P], slane[:, bass.ds(QUAD * q + (QUAD - 1), 1)],
                                    sew[:, bass.ds(QUAD * q + (QUAD - 1), 1)], ALU.is_equal, ALU.mult
                                    ).then_inc(split_ready, 1)

            def boundary(b):
                if within(b, 1):
                    v.wait_ge(x2h_ready, b)
                    v.tensor_tensor(xt_lo[:, 0], psum[:, 1].rearrange("p (k n) -> p k n", k=KD),
                                    xt_hi[:, 0].bitcast(fp32), ALU.subtract).then_inc(x2l_ready, 1)
                if within(b, 2):
                    v.wait_ge(silu_ready, b - 1)
                    if within(b, 3):
                        v.wait_ge(hT_ready, b - 2)
                    v.wait_ge(logits_ready, b - 1)
                    v.tensor_tensor(hid[:, 1], hid[:, 0], psum[:, 4], ALU.mult).then_inc(hs_ready, 1)
                if within(b, 3):
                    v.wait_ge(hTh_ready, b - 2)
                    v.tensor_tensor(sht_lo, psum[:, 5].rearrange("p (k n) -> p k n", k=KD),
                                    sht_hi.bitcast(fp32), ALU.subtract).then_inc(hTl_ready, 1)
                if within(b, 4):
                    v.wait_ge(y_ready, b - 3)
                    v.tensor_tensor(row(b - 4), row(b - 4), psum[:, 6], ALU.add).then_inc(shared_done, 1)
                if within(b, 0):
                    v.wait_ge(agg_ready, b + 1)
                    v.scalar_tensor_tensor(row(b), psum[:, 0], 0.0, row(b), ALU.max, ALU.add).then_inc(x1_done, 1)
                    sk.base, sk.n = b * NORM_STEPS, 0
                    v.wait_ge(x1_done, b + 1)
                    hold(v)
                    sk.add(v.bn_stats(stats[:, 0], row(b)))
                    sk.wait()
                    hold(v)
                    sk(v.bn_aggr(mv[:, 0], stats[:, 0]))
                    rsqrt(sk, rstd[:, 0:1], [mv[:, 0, 1:2], newton[:, 1, 0:1], newton[:, 2, 0:1]], newton[:, 3, 0:1], 1)
                    assert sk.n == NORM_STEPS, sk.n
                    if within(b, 1):
                        v.wait_ge(xn2_stored, 16 * b)
                        v.wait_ge(t2_ready, b)
                    v.tensor_scalar(xn[:, 0], row(b), mv[:, 0, 0:1], rstd[:, 0:1], ALU.subtract, ALU.mult
                                    ).then_inc(xn2_ready, 1)

            sr = Steps(v, dve_route)

            score, exp_f, rank, first_tile, valid, slot_c, slot_s, lane_f, tile_f, gate = (
                r_small[:, j] for j in range(10))
            large = ring[:, 0:HALF].rearrange("p r n -> p (r n)")
            oh_k = [large[:, 1024 * k:1024 * (k + 1)].rearrange("p (e t) -> p e t", t=TILES) for k in range(TOPK)]
            prod = large[:, 2048:3072].rearrange("p (e t) -> p e t", t=TILES)
            ranks = large[:, 3072:4096].rearrange("p (e t) -> p e t", t=TILES)
            rscan = hwb.rearrange("p s n -> p (s n)")
            oh_sum = onehot[:, 0:EXPERTS * TILES].rearrange("p (e t) -> p e t", t=TILES)
            big = [P, EXPERTS, TILES]

            def best():
                v.wait_ge(logits_ready, TILES)
                for t in range(TILES):
                    sr.add(v.max(top8[:, t], logits[:, t]))
                sr.wait()
                v.sem_inc(top_ready, 1)
                for t in range(TILES):
                    sr.add(v.max_index(idx8[:, t], top8[:, t], logits[:, t]))

                sr.wait()
                sr(v.tensor_copy(exp_f, idx8[:, :, 0:TOPK].rearrange("p t k -> p k t")))
                for k in range(TOPK):
                    sr.add(v.tensor_tensor(oh_k[k], exp_f[:, k].unsqueeze(1).to_broadcast(big),
                                           iota_f[:, 0:EXPERTS].unsqueeze(2).to_broadcast(big), ALU.is_equal))
                sr.wait()
                v.tensor_tensor(oh_sum, oh_k[0], oh_k[1], ALU.add).then_inc(pairs_oh, 1)

            blocks(v, aggregate, boundary, best)
            v.wait_ge(sig_ready, 1)
            sr(v.tensor_tensor(gate[:, 0], score[:, 0], score[:, 1], ALU.add))
            sr(v.tensor_scalar(gate[:, 0], gate[:, 0], 1e-20, None, ALU.add))
            sr(v.reciprocal(gate[:, 1], gate[:, 0]))
            sr(v.tensor_tensor(gate[:, 0], score[:, 0], gate[:, 1], ALU.mult))
            sr(v.tensor_tensor(gate[:, 1], score[:, 1], gate[:, 1], ALU.mult))
            sr(v.tensor_scalar(gate, gate, ROUTE_SCALE, None, ALU.mult))
            v.wait_ge(rtot, 1)
            for b in range(2):
                sr(v.tensor_tensor_scan(rscan[:, 512 * b:512 * b + 512], psum[:, b], zeros[:],
                                        0.0 if b == 0 else rscan[:, 511:512], ALU.add, ALU.add))
            rscan3 = rscan.rearrange("p (e t) -> p e t", t=TILES)
            e_end = rscan3[:, :, TILES - 1]
            e_cnt, e_start, e_tiles, t_end, t_start, e_tmp = (x_small[:, j] for j in range(6))
            sr.add(v.tensor_copy(e_cnt[:, 0:1], e_end[:, 0:1]))
            sr(v.tensor_tensor(e_cnt[:, 1:], e_end[:, 1:], e_end[:, 0:EXPERTS - 1], ALU.subtract))
            sr.add(v.tensor_tensor(e_start, e_end, e_cnt, ALU.subtract))
            sr(v.tensor_scalar(e_tmp, e_cnt, float(CAP), float(P - 1), ALU.min, ALU.add))
            sr(v.tensor_copy(x_int, e_tmp))
            sr(v.tensor_scalar(x_int, x_int, BLOCK_SHIFT, None, ALU.logical_shift_right))
            sr(v.tensor_copy(e_tiles, x_int))
            sr(v.tensor_tensor_scan(t_end, e_tiles, zeros[:, 0:EXPERTS], 0.0, ALU.add, ALU.add))
            sr.add(v.tensor_tensor(t_start, t_end, e_tiles, ALU.subtract))
            sr(v.tensor_scalar(x_small[:, 6], t_end, tok_f[:, 0:1], None, ALU.is_le))
            sr(v.tensor_reduce(texp_f[:, 0:1], x_small[:, 6], AX.X, ALU.add))
            v.tensor_scalar(texp_f[:, 1:2], texp_f[:, 0:1], float(EXPERTS - 1), None, ALU.min).then_inc(texp_c, 1)
            sr(v.tensor_scalar(x_small[:, 7, 0:1], t_end[:, EXPERTS - 1:EXPERTS], 1.0, None, ALU.add))
            sr(v.tensor_copy(x_int[:, 0:1], x_small[:, 7, 0:1]))
            sr(v.tensor_scalar(x_int[:, 0:1], x_int[:, 0:1], 1, None, ALU.logical_shift_right))
            sr(v.tensor_copy(x_small[:, 7, 0:1], x_int[:, 0:1]))
            sr(v.tensor_scalar(groups[:], x_small[:, 7, 0:1], -2.0, 1.0, ALU.add, ALU.max))
            v.wait_ge(texp_t, 1)
            sr(v.tensor_copy(texp_row, psum[0:1, 5, 0:P]))
            v.sem_inc(experts_known, 1)
            v.wait_ge(rpre, 1)
            sr(v.tensor_tensor(ranks, rscan3, psum[:, 2:4].rearrange("p b (e t) -> p (b e) t", t=TILES), ALU.add))
            sr(v.scalar_tensor_tensor(e_tmp, t_start, float(RANKS), e_start, ALU.mult, ALU.subtract))
            sr(v.tensor_tensor(ranks, ranks, e_tmp.unsqueeze(2).to_broadcast(big), ALU.add))
            for k in range(TOPK):
                sr(v.tensor_tensor(prod, oh_k[k], ranks, ALU.mult))
                sr(v.tensor_reduce(slot_s[:, k], prod.rearrange("p e t -> p t e"), AX.X, ALU.add))
            sr(v.tensor_copy(r_int[:, 0], slot_s))
            sr.add(v.tensor_scalar(r_int[:, 1], r_int[:, 0], RANKS - 1, None, ALU.bitwise_and))
            sr(v.tensor_scalar(r_int[:, 2], r_int[:, 0], RANK_SHIFT, None, ALU.logical_shift_right))
            sr.add(v.tensor_copy(rank, r_int[:, 1]))
            sr(v.tensor_copy(first_tile, r_int[:, 2]))
            sr(v.tensor_scalar(valid, rank, float(CAP), None, ALU.is_lt))
            sr(v.scalar_tensor_tensor(slot_c, first_tile, float(P), rank, ALU.mult, ALU.add))
            sr(v.tensor_tensor(slot_c, slot_c, valid, ALU.mult))
            sr.add(v.tensor_tensor(gate, gate, valid, ALU.mult))
            sr.add(v.tensor_copy(comb_idx[:].rearrange("p t k -> p k t"), slot_c))
            sr(v.tensor_scalar(slot_s, valid, float(-NOWHERE * P), float(NOWHERE * P), ALU.mult, ALU.add))
            sr(v.tensor_tensor(slot_s, slot_s, slot_c, ALU.add))
            sr(v.tensor_copy(r_int[:, 0], slot_s))
            sr.add(v.tensor_scalar(r_int[:, 1], r_int[:, 0], P - 1, None, ALU.bitwise_and))
            sr(v.tensor_scalar(r_int[:, 2], r_int[:, 0], BLOCK_SHIFT, None, ALU.logical_shift_right))
            sr.add(v.tensor_copy(lane_f, r_int[:, 1]))
            sr(v.tensor_copy(tile_f, r_int[:, 2]))
            with v.Fori(0, TILES // 2) as i:
                for j in range(2):
                    t = bass.ds(2 * i + j, 1)
                    for k in range(TOPK):
                        v.wait_ge(tsort_used, 2 * TOPK * i + (TOPK * j + k + 1))
                        v.tensor_scalar(lane_oh[:, j, k, 0], iota_f[:, 0:P], lane_f[:, k, t], tok_f[:, t],
                                        ALU.is_equal, ALU.mult)
                        v.tensor_scalar(tile_oh[:, j, k, 0:MAX_TILES], iota_f[:, 0:MAX_TILES], tile_f[:, k, t],
                                        None, ALU.is_equal).then_inc(tsort_ready, 1)
            v.wait_ge(tsort_used, TILES * TOPK + 2 * TOPK)
            sr(v.tensor_copy(tok_sorted, psum[:, 4, 0:MAX_TILES]))
            v.sem_inc(tables, 1)
            boundary(TILES + DRAIN - 1)
            middle = v.value_load(groups[0:1, 0:1], min_val=1, max_val=MAX_TILES // 2 - 2)

            def split13(b, c):
                s = c % 2
                v.wait_ge(w13h, b + (c + 1))
                v.tensor_tensor(w13_lo[s], w_raw[s][:, 0:KD * 2 * H], w13_hi[s].bitcast(fp32), ALU.subtract
                                ).then_inc(w13l, 1)

            def split2(b, c):
                s = c % 2
                v.wait_ge(w2h, b + (c + 1))
                v.tensor_tensor(w2_lo[s], w_raw[s][:, KD * 2 * H:], w2_hi[s].bitcast(fp32), ALU.subtract
                                ).then_inc(w2l, 1)

            def x_low(b, c):
                s = c % 2
                v.wait_ge(exh_ready, b + (c + 1))
                v.tensor_tensor(xt_lo[:, s], psum[:, s].rearrange("p (k n) -> p k n", k=KD),
                                xt_hi[:, s].bitcast(fp32), ALU.subtract).then_inc(exl_ready, 1)

            def h_low(b, c):
                s = c % 2
                v.wait_ge(ehth_ready, b + (c + 1))
                v.tensor_tensor(ht_lo[:, 2 * s:2 * s + 2, 0:P], psum[:, 4 + s, 0:H].rearrange("p (k n) -> p k n", k=KH),
                                ht_hi[:, 2 * s:2 * s + 2, 0:P].bitcast(fp32), ALU.subtract).then_inc(ehtl_ready, 1)

            def gated(b, c):
                s = c % 2
                v.wait_ge(sil_ready, b + (c + 1))
                v.tensor_tensor(hid[:, s, H:2 * H], hid[:, s, 0:H], psum[:, 2 + s, H:2 * H], ALU.mult
                                ).then_inc(eh_ready, 1)

            def step(b, c, ahead=2):
                if ahead >= 1:
                    x_low(b, c + 1)
                split2(b, c)
                gated(b, c)
                if ahead == 2:
                    split13(b, c + 2)
                h_low(b, c)

            split13(0, 0)
            split13(0, 1)
            x_low(0, 0)
            step(0, 0)
            with v.Fori(0, middle) as g:
                step(2 * g, 1)
                step(2 * g, 2)
            rest = 2 * middle
            step(rest, 1)
            step(rest, 2, ahead=1)
            step(rest, 3, ahead=0)
            per = HALF // TOPK
            with v.Fori(0, TILES * TOPK // RING) as i:
                for h in range(2):
                    for j in range(per):
                        t = 2 * per * i + (per * h + j)
                        acc_t = acc[:, bass.ds(t, 1), :].rearrange("p a n -> p (a n)")
                        v.wait_ge(yg_in[HALF * h + 2 * j], 16 * i + 16)
                        v.scalar_tensor_tensor(acc_t, yg[h][:, 2 * j], gate[:, 0, bass.ds(t, 1)], acc_t,
                                               ALU.mult, ALU.add).then_inc(comb_steps, 1)
                        v.wait_ge(comb_steps, 2 * per * i + (per * h + j + 1))
                        v.wait_ge(yg_in[HALF * h + 2 * j + 1], 16 * i + 16)
                        v.scalar_tensor_tensor(acc_t, yg[h][:, 2 * j + 1], gate[:, 1, bass.ds(t, 1)], acc_t,
                                               ALU.mult, ALU.add).then_inc(combined, 1)


_INS = ['x', 'src', 'dst', 'edge_weight', 'L0_gnn_W', 'L0_gnn_bias', 'L0_ffn_gate_w', 'L0_ffn_w1', 'L0_ffn_w3',
        'L0_ffn_w2', 'L0_ffn_sw1', 'L0_ffn_sw3', 'L0_ffn_sw2']
_OUTS = [((N, D), 'float32')]


def kernel(**inputs):
    import numpy as _np
    import concourse.bacc as _bacc
    from concourse.bass_utils import run_bass_kernel_spmd as _run

    nc = _bacc.Bacc("TRN2", target_bir_lowering=False, num_devices=1)
    arrays, args = {}, []
    for name in _INS:
        a = _np.ascontiguousarray(inputs[name])
        arrays[f"in_{name}_dram"] = a
        args.append(nc.dram_tensor(f"in_{name}_dram", a.shape, mybir.dt.from_np(a.dtype), kind="ExternalInput").ap())
    for i, (shape, dtype) in enumerate(_OUTS):
        dt = mybir.dt.from_np(_np.dtype(dtype))
        args.append(nc.dram_tensor(f"out_{i}_dram", shape, dt, kind="ExternalOutput").ap())
    build_program(nc, *args)
    r = _run(nc, [arrays], core_ids=[0])
    got = tuple(r.results[0][f"out_{i}_dram"] for i in range(len(_OUTS)))
    return got[0]
```
